# Optimizing a Trainium2 kernel written in Bass

```python
import numpy as np
import jax
import jax.numpy as jnp

def _softmax(x, axis=-1):
    return jax.nn.softmax(x, axis=axis)

def _gelu(x):
    return jax.nn.gelu(x, approximate=True)

def _silu(x):
    return jax.nn.silu(x)

def _sigmoid(x):
    return jax.nn.sigmoid(x)

def _layernorm(x, axis=-1, eps=1e-05):
    m = jnp.mean(x, axis=axis, keepdims=True)
    v = jnp.var(x, axis=axis, keepdims=True)
    return (x - m) / jnp.sqrt(v + eps)

def _scatter_add(tgt, idx, src, axis=0):
    return tgt.at[idx].add(src)

def _segment_sum(src, seg, n):
    return jax.ops.segment_sum(src, seg, n)
kernel_name = 'mk_flamingo_gated_d2_seqx_r2_6cba73'

def setup_inputs(seed: int=0):
    np.random.seed(seed)
    _w = jnp.asarray

    def _rec_inputs():
        import jax
        import jax.numpy as jnp
        _rk = jax.random.key(seed)
        x = -0.0002928 + 1 * jax.random.normal(jax.random.fold_in(_rk, 1), (8, 512, 512), jnp.float32)
        _lenS = 512 - jax.random.randint(jax.random.fold_in(_rk, 7), (8,), 0, max(1, 512 // 4) + 1, jnp.int32)
        _lenS2 = 120 - jax.random.randint(jax.random.fold_in(_rk, 8), (8,), 0, max(1, 120 // 4) + 1, jnp.int32)
        _ctx_1024P = jax.random.normal(jax.random.fold_in(_rk, 11), (8, 16, 512), jnp.float32)
        _ctx_1024c = jax.random.dirichlet(jax.random.fold_in(_rk, 511), 0.3 * jnp.ones((16,), jnp.float32), (8, 120))
        _ctx_1024t = jnp.einsum('bsk,bkd->bsd', _ctx_1024c, _ctx_1024P)
        _ctx_1024t = _ctx_1024t * jax.lax.rsqrt(jnp.mean(jnp.square(_ctx_1024t)) + 1e-12) * 0.953939
        ctx_1024 = -1.39393e-06 + 0.999914 * (_ctx_1024t + 0.3 * jax.random.normal(jax.random.fold_in(_rk, 611), (8, 120, 512), jnp.float32))
        itok_BxS_0_511 = jax.random.randint(jax.random.fold_in(_rk, 12), (8, 512), 0, 256, jnp.int32)
        _g = jax.random.normal(jax.random.fold_in(_rk, 9001), (2, 2), jnp.float32)
        _g = jnp.sign(_g) * jnp.maximum(jnp.abs(_g), 1.0) + (_g == 0) * 1.0
        g_xattn = _g[0]
        g_ffn = _g[1]
        return (x, ctx_1024, itok_BxS_0_511, g_xattn, g_ffn)
    x, ctx_1024, itok_BxS_0_511, g_xattn, g_ffn = _rec_inputs()

    def _L0_xattn_setup():
        import jax, jax.numpy as jnp
        import numpy as np
        NUM_HEADS = 16
        SPARSITY = 0.1
        key = jax.random.key(seed)
        ks = jax.random.split(key, 11)
        B, S, D = (2, 1024, 512)
        s = 0.02
        return {'query': jax.random.normal(ks[0], (B, S, D), jnp.float32), 'key': jax.random.normal(ks[1], (B, S, D), jnp.float32), 'value': jax.random.normal(ks[2], (B, S, D), jnp.float32), 'Wq': jax.random.normal(ks[3], (D, D), jnp.float32) * s, 'bq': jax.random.normal(ks[4], (D,), jnp.float32) * s, 'Wk': jax.random.normal(ks[5], (D, D), jnp.float32) * s, 'bk': jax.random.normal(ks[6], (D,), jnp.float32) * s, 'Wv': jax.random.normal(ks[7], (D, D), jnp.float32) * s, 'bv': jax.random.normal(ks[8], (D,), jnp.float32) * s, 'Wo': jax.random.normal(ks[9], (D, D), jnp.float32) * s, 'bo': jax.random.normal(ks[10], (D,), jnp.float32) * s}
    _L0_xattn_all = _L0_xattn_setup()
    _L0_xattn_in = {k: v for k, v in _L0_xattn_all.items() if k in ('Wq', 'bq', 'Wk', 'bk', 'Wv', 'bv', 'Wo', 'bo')}
    del _L0_xattn_all

    def _L0_ffn_setup():
        import jax, jax.numpy as jnp
        import numpy as np
        NUM_EXPERTS = 8
        D_MODEL = 512
        D_FF = 2048
        BATCH, SEQ = (2, 2048)
        key = jax.random.key(seed)
        k_x, k_w1, k_w2 = jax.random.split(key, 3)
        x = jax.random.normal(k_x, (BATCH, SEQ, D_MODEL), dtype=jnp.float32)
        w1 = jax.random.normal(k_w1, (NUM_EXPERTS, D_MODEL, D_FF), dtype=jnp.float32) * (1.0 / np.sqrt(D_MODEL))
        b1 = jnp.zeros((NUM_EXPERTS, D_FF), dtype=jnp.float32)
        w2 = jax.random.normal(k_w2, (NUM_EXPERTS, D_FF, D_MODEL), dtype=jnp.float32) * (1.0 / np.sqrt(D_FF))
        b2 = jnp.zeros((NUM_EXPERTS, D_MODEL), dtype=jnp.float32)
        return {'x': x, 'w1': w1, 'b1': b1, 'w2': w2, 'b2': b2}
    _L0_ffn_all = _L0_ffn_setup()
    _L0_ffn_in = {k: v for k, v in _L0_ffn_all.items() if k in ('w1', 'b1', 'w2', 'b2')}
    del _L0_ffn_all

    def _L1_xattn_setup():
        import jax, jax.numpy as jnp
        import numpy as np
        Q_DIM, KV_DIM = (512, 512)
        H, HD, KVC, QC, R = (16, 64, 128, 192, 64)
        LOOKBACK = 2
        B, LQ, LK = (4, 1024, 256)

        def _rope(x, pos):
            r = x.shape[-1]
            half = r // 2
            inv = 1.0 / 10000.0 ** (jnp.arange(half, dtype=jnp.float32) / half)
            ang = pos[..., None].astype(jnp.float32) * inv
            cos, sin = (jnp.cos(ang), jnp.sin(ang))
            x1, x2 = (x[..., :half], x[..., half:])
            return jnp.concatenate([x1 * cos - x2 * sin, x1 * sin + x2 * cos], axis=-1)
        key = jax.random.key(seed)
        ks = jax.random.split(key, 11)
        w = lambda k, shape: jax.random.normal(k, shape, jnp.float32) / np.sqrt(shape[0]).astype(np.float32)
        return {'q': jax.random.normal(ks[0], (B, LQ, Q_DIM), jnp.float32), 'kv': jax.random.normal(ks[1], (B, LK, KV_DIM), jnp.float32), 'seg_id': jnp.sort(jax.random.randint(ks[2], (B, LQ), 0, LK), axis=-1), 'w_kv_comp': w(ks[3], (KV_DIM, KVC)), 'w_q_down': w(ks[4], (Q_DIM, QC)), 'w_q_up': w(ks[5], (QC, H * HD)), 'w_q_rope': w(ks[6], (QC, H * R)), 'w_k_up': w(ks[7], (KVC, H * HD)), 'w_k_rope': w(ks[8], (KVC, R)), 'w_v_up': w(ks[9], (KVC, H * HD)), 'w_out': w(ks[10], (H * HD, Q_DIM))}
    _L1_xattn_all = _L1_xattn_setup()
    _L1_xattn_in = {k: v for k, v in _L1_xattn_all.items() if k in ('w_kv_comp', 'w_q_down', 'w_q_up', 'w_q_rope', 'w_k_up', 'w_k_rope', 'w_v_up', 'w_out')}
    del _L1_xattn_all

    def _L1_ffn_setup():
        import jax, jax.numpy as jnp
        import numpy as np

        def _bitlinear(x, w_latent):
            scale = jax.lax.stop_gradient(jnp.clip(jnp.mean(jnp.abs(w_latent), axis=1, keepdims=True), 1e-05, None))
            tern = jnp.clip(jnp.round(w_latent / scale), -1.0, 1.0)
            w = w_latent + jax.lax.stop_gradient(tern - w_latent)
            return x @ (w * scale).T
        key = jax.random.key(seed)
        ks = jax.random.split(key, 6)
        dim, hidden, rank = (512, 2048, 16)
        B, S = (4, 2048)
        x = jax.random.normal(ks[0], (B, S, dim), dtype=jnp.float32)
        w_fc = 0.02 * jax.random.normal(ks[1], (hidden, dim), dtype=jnp.float32)
        w_proj = 0.02 * jax.random.normal(ks[2], (dim, hidden), dtype=jnp.float32)
        u = 0.02 * jax.random.normal(ks[3], (hidden, rank), dtype=jnp.float32)
        v = 0.02 * jax.random.normal(ks[4], (rank, dim), dtype=jnp.float32)
        fast_b = jax.random.normal(ks[5], (rank, rank), dtype=jnp.float32)
        gate = jnp.float32(0.05)
        return {'x': x, 'fast_b': fast_b, 'w_fc': w_fc, 'w_proj': w_proj, 'u': u, 'v': v, 'gate': gate}
    _L1_ffn_all = _L1_ffn_setup()
    _L1_ffn_in = {k: v for k, v in _L1_ffn_all.items() if k in ('fast_b', 'w_fc', 'w_proj', 'u', 'v', 'gate')}
    del _L1_ffn_all
    return {'x': x, 'ctx_1024': ctx_1024, 'itok_BxS_0_511': itok_BxS_0_511, 'g_xattn': g_xattn, 'g_ffn': g_ffn, 'L0_xattn_Wq': _L0_xattn_in['Wq'], 'L0_xattn_bq': _L0_xattn_in['bq'], 'L0_xattn_Wk': _L0_xattn_in['Wk'], 'L0_xattn_bk': _L0_xattn_in['bk'], 'L0_xattn_Wv': _L0_xattn_in['Wv'], 'L0_xattn_bv': _L0_xattn_in['bv'], 'L0_xattn_Wo': _L0_xattn_in['Wo'], 'L0_xattn_bo': _L0_xattn_in['bo'], 'L0_ffn_w1': _L0_ffn_in['w1'], 'L0_ffn_b1': _L0_ffn_in['b1'], 'L0_ffn_w2': _L0_ffn_in['w2'], 'L0_ffn_b2': _L0_ffn_in['b2'], 'L1_xattn_w_kv_comp': _L1_xattn_in['w_kv_comp'], 'L1_xattn_w_q_down': _L1_xattn_in['w_q_down'], 'L1_xattn_w_q_up': _L1_xattn_in['w_q_up'], 'L1_xattn_w_q_rope': _L1_xattn_in['w_q_rope'], 'L1_xattn_w_k_up': _L1_xattn_in['w_k_up'], 'L1_xattn_w_k_rope': _L1_xattn_in['w_k_rope'], 'L1_xattn_w_v_up': _L1_xattn_in['w_v_up'], 'L1_xattn_w_out': _L1_xattn_in['w_out'], 'L1_ffn_fast_b': _L1_ffn_in['fast_b'], 'L1_ffn_w_fc': _L1_ffn_in['w_fc'], 'L1_ffn_w_proj': _L1_ffn_in['w_proj'], 'L1_ffn_u': _L1_ffn_in['u'], 'L1_ffn_v': _L1_ffn_in['v'], 'L1_ffn_gate': _L1_ffn_in['gate']}

def reference(x, ctx_1024, itok_BxS_0_511, g_xattn, g_ffn, L0_xattn_Wq, L0_xattn_bq, L0_xattn_Wk, L0_xattn_bk, L0_xattn_Wv, L0_xattn_bv, L0_xattn_Wo, L0_xattn_bo, L0_ffn_w1, L0_ffn_b1, L0_ffn_w2, L0_ffn_b2, L1_xattn_w_kv_comp, L1_xattn_w_q_down, L1_xattn_w_q_up, L1_xattn_w_q_rope, L1_xattn_w_k_up, L1_xattn_w_k_rope, L1_xattn_w_v_up, L1_xattn_w_out, L1_ffn_fast_b, L1_ffn_w_fc, L1_ffn_w_proj, L1_ffn_u, L1_ffn_v, L1_ffn_gate):
    import jax
    import jax.numpy as jnp

    def _L0_xattn_ref(query, key, value, Wq, bq, Wk, bk, Wv, bv, Wo, bo):
        import jax, jax.numpy as jnp
        import numpy as np
        NUM_HEADS = 16
        SPARSITY = 0.1
        B, Q, D = query.shape
        K = key.shape[1]
        H = NUM_HEADS
        hd = D // H
        scale = 1.0 / np.sqrt(hd).astype(np.float32)
        q = (query @ Wq.T + bq).reshape(B, Q, H, hd).transpose(0, 2, 1, 3)
        k = (key @ Wk.T + bk).reshape(B, K, H, hd).transpose(0, 2, 1, 3)
        v = (value @ Wv.T + bv).reshape(B, K, H, hd).transpose(0, 2, 1, 3)
        rel = jnp.einsum('bhqd,bhkd->bhqk', q, k) * scale
        k_per_query = max(1, int(K * SPARSITY))
        top_rel = jax.lax.top_k(rel, k_per_query)[0]
        threshold = top_rel[..., -1:]
        attn = jnp.where(rel < threshold, -jnp.inf, rel)
        attn = jax.nn.softmax(attn, axis=-1)
        out = jnp.einsum('bhqk,bhkd->bhqd', attn, v)
        out = out.transpose(0, 2, 1, 3).reshape(B, Q, D)
        return out @ Wo.T + bo

    def _L0_ffn_ref(x, w1, b1, w2, b2):
        import jax, jax.numpy as jnp
        import numpy as np
        NUM_EXPERTS = 8
        D_MODEL = 512
        D_FF = 2048
        BATCH, SEQ = (2, 2048)
        B, S, D = x.shape
        E = w1.shape[0]
        T = B * S // E
        tokens = x.reshape(E, T, D)
        h = jnp.einsum('etd,edf->etf', tokens, w1) + b1[:, None, :]
        h = jax.nn.gelu(h)
        y = jnp.einsum('etf,efd->etd', h, w2) + b2[:, None, :]
        return y.reshape(B, S, D)

    def _L1_xattn_ref(q, kv, seg_id, w_kv_comp, w_q_down, w_q_up, w_q_rope, w_k_up, w_k_rope, w_v_up, w_out):
        import jax, jax.numpy as jnp
        import numpy as np
        Q_DIM, KV_DIM = (512, 512)
        H, HD, KVC, QC, R = (16, 64, 128, 192, 64)
        LOOKBACK = 2
        B, LQ, LK = (4, 1024, 256)

        def _rope(x, pos):
            r = x.shape[-1]
            half = r // 2
            inv = 1.0 / 10000.0 ** (jnp.arange(half, dtype=jnp.float32) / half)
            ang = pos[..., None].astype(jnp.float32) * inv
            cos, sin = (jnp.cos(ang), jnp.sin(ang))
            x1, x2 = (x[..., :half], x[..., half:])
            return jnp.concatenate([x1 * cos - x2 * sin, x1 * sin + x2 * cos], axis=-1)
        b, lq, _ = q.shape
        lk = kv.shape[1]
        kv_c = kv @ w_kv_comp
        qc = q @ w_q_down
        q_nope = (qc @ w_q_up).reshape(b, lq, H, HD)
        q_rope = (qc @ w_q_rope).reshape(b, lq, H, R)
        q_rope = _rope(q_rope, jnp.arange(lq)[None, :, None])
        k_nope = (kv_c @ w_k_up).reshape(b, lk, H, HD)
        k_rope = _rope(kv_c @ w_k_rope, jnp.arange(lk)[None, :])
        v = (kv_c @ w_v_up).reshape(b, lk, H, HD)
        scale = 1.0 / np.sqrt(HD + R).astype(np.float32)
        scores = (jnp.einsum('bqhd,bkhd->bhqk', q_nope, k_nope) + jnp.einsum('bqhr,bkr->bhqk', q_rope, k_rope)) * scale
        k_idx = jnp.arange(lk)[None, None, :]
        q_seg = seg_id[:, :, None]
        good = (k_idx <= q_seg) & (k_idx >= q_seg - LOOKBACK)
        neg = jnp.finfo(scores.dtype).min
        scores = jnp.where(good[:, None, :, :], scores, neg)
        attn = jax.nn.softmax(scores, axis=-1)
        out = jnp.einsum('bhqk,bkhd->bqhd', attn, v).reshape(b, lq, H * HD)
        return out @ w_out

    def _L1_ffn_ref(x, fast_b, w_fc, w_proj, u, v, gate):
        import jax, jax.numpy as jnp
        import numpy as np

        def _bitlinear(x, w_latent):
            scale = jax.lax.stop_gradient(jnp.clip(jnp.mean(jnp.abs(w_latent), axis=1, keepdims=True), 1e-05, None))
            tern = jnp.clip(jnp.round(w_latent / scale), -1.0, 1.0)
            w = w_latent + jax.lax.stop_gradient(tern - w_latent)
            return x @ (w * scale).T
        h = _bitlinear(x, w_fc) + gate * (x @ v.T @ fast_b.T @ u.T)
        r = jnp.maximum(h, 0.0)
        return _bitlinear(r * r, w_proj)
    x = x + jnp.tanh(g_xattn[0]) * _L0_xattn_ref(_layernorm(x, axis=-1), ctx_1024, ctx_1024, L0_xattn_Wq, L0_xattn_bq, L0_xattn_Wk, L0_xattn_bk, L0_xattn_Wv, L0_xattn_bv, L0_xattn_Wo, L0_xattn_bo)
    x = x + jnp.tanh(g_ffn[0]) * _L0_ffn_ref(_layernorm(x, axis=-1), L0_ffn_w1, L0_ffn_b1, L0_ffn_w2, L0_ffn_b2)
    x = x + jnp.tanh(g_xattn[1]) * _L1_xattn_ref(_layernorm(x, axis=-1), ctx_1024, itok_BxS_0_511, L1_xattn_w_kv_comp, L1_xattn_w_q_down, L1_xattn_w_q_up, L1_xattn_w_q_rope, L1_xattn_w_k_up, L1_xattn_w_k_rope, L1_xattn_w_v_up, L1_xattn_w_out)
    x = x + jnp.tanh(g_ffn[1]) * _L1_ffn_ref(_layernorm(x, axis=-1), L1_ffn_fast_b, L1_ffn_w_fc, L1_ffn_w_proj, L1_ffn_u, L1_ffn_v, L1_ffn_gate)
    return x

_drawn_inputs = setup_inputs


def setup_inputs(seed=0):
    import zlib

    import numpy as np

    out = dict(_drawn_inputs(seed))
    spreads = {'g_ffn': (-1.0, 0.6), 'L0_ffn_b1': (0.0, 0.1), 'L0_ffn_b2': (0.0, 0.1)}
    factors = {'L0_xattn_bq': 7.172,
     'L0_xattn_bk': 8.0,
     'L0_xattn_bv': 8.0,
     'L0_xattn_bo': 4.05,
     'L1_ffn_fast_b': 8.0,
     'L1_ffn_u': 8.0,
     'L1_ffn_v': 8.0}
    for name, (base, spread) in spreads.items():
        noise = np.random.default_rng([zlib.crc32(name.encode()), seed]).standard_normal(out[name].shape)
        drawn = base * np.exp(spread * noise) if base else spread * noise
        out[name] = jnp.asarray(drawn.astype(out[name].dtype))
    for name, factor in factors.items():
        out[name] = (out[name] * factor).astype(out[name].dtype)
    return out
```

```python
from contextlib import ExitStack

import numpy as np

import concourse.bass as bass
from concourse import mybir

ALU = mybir.AluOpType
ACT = mybir.ActivationFunctionType
F32 = mybir.dt.float32
F16 = mybir.dt.float16
I32 = mybir.dt.int32
AX_X = mybir.AxisListType.X

P = 128
B = 8
S = 512
D = 512
NT = S // P
NK = D // P
KEYS = 120
EPS = 1e-5
WS = 64.0
LOWEST = -3.4028234663852886e38

H = 16
HD0 = D // H
HG = 4
NG = H // HG
STEPS = NT * NG
SLOTS = STEPS + 10
TOP = max(1, int(KEYS * 0.1))
EXP0 = float(1.0 / np.sqrt(np.float32(HD0))) / (WS * WS)
F = 2048
NM = F // P
NW = 3
HD = 64
R = 64
KVC = 128
QC = 192
QR = QC - P
LOOKBACK = 2
EXP1 = float(1.0 / np.sqrt(np.float32(HD + R))) / (WS * WS)
RANK = 16
ROUND = 12582912.0
ZROWS = 96


class Signal:

    def __init__(self, nc, ctx, name, per):
        self.sem = ctx.enter_context(nc.semaphore(name))
        self.per = per

    def at(self, b, n):
        return b * self.per + (n + 1)


class Chain:

    def __init__(self, sem):
        self.sem, self.n = sem, 0

    def add(self, ins):
        self.n += 1
        ins.then_inc(self.sem, 1)
        return self.n


def prime(eng, signals):
    for s in signals:
        eng.sem_inc(s.sem, 1)


def wait(eng, s, b, n):
    eng.wait_ge(s.sem, s.at(b, n))


def layer0(nc, io):
    DVE_LINKS = 52
    with ExitStack() as ctx:
        sb = lambda name, shape, dt=F32: ctx.enter_context(nc.sbuf_tensor(name, shape, dt))
        pb = lambda name, dt=F32: ctx.enter_context(nc.psum_tensor(name, [P, 512], dt))
        sem = lambda name: ctx.enter_context(nc.semaphore(name))
        sig = lambda name, per: Signal(nc, ctx, name, per)

        wq = [sb(f"wq{h}", [P, NK, D], F16) for h in "hl"]
        wk = [sb(f"wk{h}", [P, NK, D], F16) for h in "hl"]
        wv = [sb(f"wv{h}", [P, NK, D], F16) for h in "hl"]
        wo = [sb(f"wo{h}", [P, NK, D], F16) for h in "hl"]
        wstage = [sb(f"wstage{i}", [P, NK, D]) for i in range(2)]
        ident = sb("ident", [P, P])
        gates = sb("gates", [P, 4])
        gt = sb("gt", [P, 4])
        gs = sb("gs", [P, 4])
        bq = sb("bq", [P, NG])
        bk = sb("bk", [P, NG])
        bv = sb("bv", [P, D])
        gbo = sb("gbo", [P, D])
        half = sb("half", [P, 1])

        xin = sb("xin", [P, NT, D])
        xa = sb("xa", [P, NT, D])
        xr = sb("xr", [P, NT, D])
        xn = [sb(f"xn{i}", [P, D]) for i in range(2)]
        stat = sb("stat", [P, 8, 6])
        mean = sb("mean", [P, 8, 2])
        vare = sb("vare", [P, 8])
        rstd = sb("rstd", [P, 8])
        xt = [sb(f"xt{h}", [P, NK, S], F16) for h in "hl"]

        cx = sb("cx", [P, D])
        cxt = [sb(f"cxt{h}", [P, NK, KEYS], F16) for h in "hl"]
        kf = sb("kf", [P, NG, KEYS])
        kb = [sb(f"kb{h}", [P, NG, HG, KEYS], F16) for h in "hl"]
        v = sb("v", [P, D])
        qt = [sb(f"qt{h}", [P, NG, S], F16) for h in "hl"]
        sc = [sb(f"sc{i}", [P, HG, KEYS]) for i in range(3)]
        ex = [sb(f"ex{i}", [P, HG, KEYS]) for i in range(2)]
        pr = [sb(f"pr{i}", [P, HG, KEYS]) for i in range(2)]
        rep = sb("rep", [P, HG, KEYS])
        top1 = [sb(f"top1{i}", [P, HG, 8]) for i in range(3)]
        top2 = [sb(f"top2{i}", [P, HG, 8]) for i in range(3)]
        rsum = sb("rsum", [P, NT, H])
        rinv = sb("rinv", [P, NT, H])
        pt = [sb(f"pt{i}", [P, HG, P]) for i in range(2)]
        ao = sb("ao", [P, D])
        aot = [sb(f"aot{h}", [P, NK, P], F16) for h in "hl"]

        b1 = sb("b1", [P, NM])
        b2 = sb("b2", [P, D])
        gb2 = sb("gb2", [P, D])
        wr = [sb(f"wr{i}", [P, 2 * D]) for i in range(2)]
        wx = [[sb(f"wx{i}{h}", [P, 2 * D], F16) for h in "hl"] for i in range(NW)]
        hf = [sb(f"hf{i}", [P, S]) for i in range(2)]
        hx = [[sb(f"hx{i}{h}", [P, S], F16) for h in "hl"] for i in range(2)]

        bT = [pb("bT0"), pb("bT1")]
        bM = [pb("bM0"), pb("bM1")]
        bP, bU, bO, bY = pb("bP"), pb("bU"), pb("bO"), pb("bY")
        acc = [bP, bU, bO, bY]

        s_const = sem("s_const")
        s_w = [sem("s_w0"), sem("s_w1")]
        s_whi = sem("s_whi")
        s_wlo = sem("s_wlo")
        s_id0 = sem("s_id0")
        s_setup = sem("s_setup")
        s_tanh = sem("s_tanh")
        s_bias = sem("s_bias")
        ld_x, ld_c, ld_b = sem("ld_x"), sem("ld_c"), sem("ld_b")
        ld_w = [sem("ld_w0"), sem("ld_w1")]
        cxt_ps, k_ps, v_ps = sig("cxt_ps", 1), sig("k_ps", 1), sig("v_ps", 1)
        xt_ps, q_ps, s_ps, pt_ps = sig("xt_ps", 2 * NT), sig("q_ps", NG), sig("s_ps", STEPS), sig("pt_ps", STEPS)
        o_ps, ao_ps, y_ps = sig("o_ps", STEPS), sig("ao_ps", NT), sig("y_ps", NT)
        h_ps, m_ps, z_ps = sig("h_ps", NM), sig("m_ps", NM - 1), sig("z_ps", NT)
        cx_hi, k_hi, q_hi, x_hi = sig("cx_hi", 1), sig("k_hi", 1), sig("q_hi", NG), sig("x_hi", 2 * NT)
        s_copy, e_done, pt_copy, ao_hi = sig("s_copy", STEPS), sig("e_done", STEPS), sig("pt_copy", STEPS), sig("ao_hi", NT)
        w_hi, gelu_done = sig("w_hi", NM), sig("gelu_done", NM)
        cx_lo, k_full, k_lo, v_done = sig("cx_lo", 1), sig("k_full", 1), sig("k_lo", 1), sig("v_done", 1)
        q_lo, x_lo, var_done, xn_done = sig("q_lo", NG), sig("x_lo", 2 * NT), sig("var_done", 2 * NT), sig("xn_done", 2 * NT)
        top_done, p_done, o_norm, ao_lo = sig("top_done", STEPS), sig("p_done", STEPS), sig("o_norm", NT), sig("ao_lo", NT)
        res1, res2 = sig("res1", NT), sig("res2", NT)
        w_lo, h_hi, h_lo = sig("w_lo", NM), sig("h_hi", NM), sig("h_lo", NM)
        dv = sig("dv", DVE_LINKS)
        shifted, rstd_done, xa_done = sig("shifted", STEPS), sig("rstd_done", 2 * NT), sig("xa_done", 2)
        gb2_done = sig("gb2_done", 1)
        x_out = sig("x_out", 16)

        block = ctx.enter_context(nc.Block())
        x_v = io["x"].rearrange("b (t p) d -> b p t d", p=P)
        mid_v = io["mid"].rearrange("b (t p) d -> b p t d", p=P)
        STAGED = [(io["L0_xattn_Wk"], wk), (io["L0_xattn_Wv"], wv), (io["L0_xattn_Wq"], wq), (io["L0_xattn_Wo"], wo)]

        @block.sync
        def _(sp):
            for n, (src, _) in enumerate(STAGED):
                if n >= 2:
                    sp.wait_ge(s_wlo, n - 1)
                sp.dma_start(wstage[n % 2][:], src.rearrange("(k p) n -> p k n", p=P)).then_inc(s_w[n % 2], 16)
            with sp.Fori(0, B) as b:
                wait(sp, xn_done, b, 0)
                wait(sp, xa_done, b, 0)
                sp.dma_start(xin[:], x_v[b]).then_inc(ld_x, 16)
                sp.dma_start(cx[0:KEYS, :], io["ctx_1024"][b]).then_inc(ld_c, 16)
                wait(sp, gelu_done, b, 0)
                sp.dma_start(b1[:], io["L0_ffn_b1"][b]).then_inc(ld_b, 16)
                wait(sp, gb2_done, b, 0)
                sp.dma_start(b2[:], io["L0_ffn_b2"][b].partition_broadcast(P)).then_inc(ld_b, 16)
                for m in range(NM):
                    wait(sp, w_lo, b, max(m - 1, 0))
                    sp.dma_start(wr[m % 2][:], io["w12"][b, m]).then_inc(ld_w[m % 2], 16)

        @block.gpsimd
        def _(pool):
            prime(pool, [shifted, rstd_done, xa_done, gb2_done])
            for dst, src in ((gates[:, 0:2], io["g_xattn"]), (gates[:, 2:4], io["g_ffn"]), (bv[:], io["L0_xattn_bv"]),
                             (gbo[:], io["L0_xattn_bo"])):
                pool.dma_start(dst, src.partition_broadcast(P)).then_inc(s_const, 16)
            pool.dma_start(bq[:], io["L0_xattn_bq"]).then_inc(s_const, 16)
            pool.dma_start(bk[:], io["L0_xattn_bk"]).then_inc(s_const, 16)
            nc.gpsimd.memset(ident[:], 0.0).then_inc(s_id0, 1)
            nc.gpsimd.memset(kb[0][:], 0.0).then_inc(s_id0, 1)
            nc.gpsimd.memset(kb[1][:], 0.0).then_inc(s_id0, 1)
            nc.gpsimd.memset(half[:], -0.5).then_inc(s_id0, 1)
            pool.wait_ge(s_id0, 4)
            nc.gpsimd.affine_select(out=ident[:], in_=ident[:], compare_op=ALU.not_equal, fill=1.0, base=0,
                                    pattern=[[-1, P]], channel_multiplier=1).then_inc(s_setup, 1)
            pool.wait_ge(s_bias, 4)
            with pool.Fori(0, B) as b:
                def power(n):
                    wait(pool, var_done, b, n + 1)
                    nc.gpsimd.tensor_tensor(rstd[:, n:n + 1], vare[:, n:n + 1], half[:], ALU.pow).then_inc(rstd_done.sem, 1)

                for t in range(NT):
                    power(t)
                pool.wait_ge(ld_x, b * 16 + 16)
                wait(pool, res2, b, 0)
                nc.gpsimd.tensor_tensor(xa[:], xin[:], gbo[:].unsqueeze(1).to_broadcast([P, NT, D]), ALU.add)\
                    .then_inc(xa_done.sem, 1)
                pool.wait_ge(ld_b, b * 32 + 32)
                nc.gpsimd.tensor_tensor(gb2[:], b2[:], gt[:, 2:3].to_broadcast([P, D]), ALU.mult).then_inc(gb2_done.sem, 1)
                for s in range(SLOTS):
                    if s < STEPS:
                        wait(pool, top_done, b, s + 1)
                        if s >= 2:
                            wait(pool, p_done, b, s - 1)
                        nc.gpsimd.tensor_tensor(ex[s % 2][:], sc[s % 3][:],
                                                top1[s % 3][:, :, 0:1].to_broadcast([P, HG, KEYS]), ALU.subtract)\
                            .then_inc(shifted.sem, 1)
                    if s % 4 == 2 and 0 <= (s - 10) // 4 < NT:
                        power(NT + (s - 10) // 4)
                wait(pool, res1, b, NT)
                wait(pool, gb2_done, b, 1)
                nc.gpsimd.tensor_tensor(xa[:], xr[:], gb2[:].unsqueeze(1).to_broadcast([P, NT, D]), ALU.add)\
                    .then_inc(xa_done.sem, 1)

        @block.scalar
        def _(act):
            prime(act, [cx_hi, k_hi, q_hi, x_hi, s_copy, e_done, pt_copy, ao_hi, w_hi, gelu_done])
            act.sem_inc(x_out.sem, 1)
            act.wait_ge(s_const, 96)
            nc.scalar.activation(gt[:], gates[:], ACT.Tanh).then_inc(s_tanh, 1)
            for n, (_, w) in enumerate(STAGED):
                act.wait_ge(s_w[n % 2], 16 * (n // 2 + 1))
                nc.scalar.activation(w[0][:], wstage[n % 2][:], ACT.Copy, scale=WS).then_inc(s_whi, 1)
            with act.Fori(0, B) as b:
                wait(act, cxt_ps, b, 1)
                nc.scalar.activation(cxt[0][:], bT[0][:, 0:NK * KEYS].rearrange("p (k n) -> p k n", k=NK), ACT.Copy)\
                    .then_inc(cx_hi.sem, 1)

                def x_high(n):
                    wait(act, xt_ps, b, n + 1)
                    if n == NT:
                        wait(act, q_ps, b, NG)
                    t, u = n % NT, (1 + n if n < NT else 1)
                    nc.scalar.activation(xt[0][:, :, t * P:(t + 1) * P], bT[u % 2][:].rearrange("p (k n) -> p k n", k=NK),
                                         ACT.Copy).then_inc(x_hi.sem, 1)

                wait(act, k_full, b, 1)
                for j in range(HG):
                    r = slice(j * HD0, (j + 1) * HD0)
                    ins = nc.scalar.activation(kb[0][r, :, j, :], kf[r, :, :], ACT.Copy)
                ins.then_inc(k_hi.sem, 1)
                for t in range(NT):
                    x_high(t)
                for g in range(NG):
                    wait(act, q_ps, b, g + 1)
                    nc.scalar.activation(qt[0][:, g, :], bM[g % 2][:], ACT.Identity, bias=bq[:, g:g + 1])\
                        .then_inc(q_hi.sem, 1)
                for s in range(SLOTS):
                    if s < STEPS:
                        wait(act, s_ps, b, s + 1)
                        if s >= 3:
                            wait(act, p_done, b, s - 2)
                        nc.scalar.activation(sc[s % 3][:], bM[s % 2][:, 0:HG * KEYS].rearrange("p (h n) -> p h n", h=HG),
                                             ACT.Copy).then_inc(s_copy.sem, 1)
                    if 1 <= s <= STEPS:
                        wait(act, shifted, b, s)
                        e = ex[(s - 1) % 2]
                        nc.scalar.activation(e[:], e[:], ACT.Exp, scale=EXP0).then_inc(e_done.sem, 1)
                    if 2 <= s < STEPS + 2:
                        i = s - 2
                        wait(act, pt_ps, b, i + 1)
                        if i >= 2:
                            wait(act, o_ps, b, i - 1)
                        nc.scalar.activation(pt[i % 2][0:KEYS], bP[0:KEYS, :].rearrange("p (h n) -> p h n", h=HG), ACT.Copy)\
                            .then_inc(pt_copy.sem, 1)
                    if s % 4 == 0 and 0 <= (s - 8) // 4 < NT:
                        t = (s - 8) // 4
                        wait(act, ao_ps, b, t + 1)
                        if t:
                            wait(act, y_ps, b, t)
                        nc.scalar.activation(aot[0][:], bT[0][:].rearrange("p (k n) -> p k n", k=NK), ACT.Copy)\
                            .then_inc(ao_hi.sem, 1)
                    if s % 4 == 1 and 0 <= (s - 13) // 4 < NT:
                        x_high(NT + (s - 13) // 4)

                def w_high(m):
                    act.wait_ge(ld_w[m % 2], b * (16 * NM // 2) + 16 * (m // 2 + 1))
                    if m >= NW:
                        wait(act, m_ps, b, m - NW + 1)
                    nc.scalar.activation(wx[m % NW][0][:], wr[m % 2][:], ACT.Copy, scale=WS).then_inc(w_hi.sem, 1)

                w_high(0)
                w_high(1)
                for m in range(NM):
                    wait(act, h_ps, b, m + 1)
                    if m >= 2:
                        wait(act, h_lo, b, m - 1)
                    nc.scalar.activation(hf[m % 2][:], bM[m % 2][:], ACT.Gelu_apprx_tanh, bias=b1[:, m:m + 1], scale=1 / WS)\
                        .then_inc(gelu_done.sem, 1)
                    if m + 2 < NM:
                        w_high(m + 2)
                wait(act, res2, b, NT)
                act.dma_start(mid_v[b], xr[:]).then_inc(x_out.sem, 16)
            act.wait_ge(x_out.sem, B * 16 + 1)

        @block.tensor
        def _(pe):
            prime(pe, [cxt_ps, k_ps, v_ps, xt_ps, q_ps, s_ps, pt_ps, o_ps, ao_ps, y_ps, h_ps, m_ps, z_ps])
            mm = nc.tensor.matmul

            def product(out, lhs, rhs, k, n):
                mm(out, lhs(0), rhs(0), start=(k == 0), stop=False)
                mm(out, lhs(0), rhs(1), start=False, stop=False)
                return mm(out, lhs(1), rhs(0), start=False, stop=(k == n - 1))

            pe.wait_ge(s_setup, 1)
            pe.wait_ge(s_bias, 4)
            pe.wait_ge(s_wlo, len(STAGED))
            with pe.Fori(0, B) as b:
                pe.wait_ge(ld_c, b * 16 + 16)
                wait(pe, cx_lo, b, 0)
                for k in range(NK):
                    ins = nc.tensor.transpose(bT[0][:, k * KEYS:(k + 1) * KEYS], cx[0:KEYS, k * P:(k + 1) * P],
                                              ident[0:KEYS, 0:KEYS])
                ins.then_inc(cxt_ps.sem, 1)

                def x_transpose(n):
                    u = 1 + n if n < NT else 1
                    wait(pe, xn_done, b, n + 1)
                    if u == 2:
                        wait(pe, cx_lo, b, 1)
                    elif n >= 2:
                        wait(pe, x_lo, b, n - 1 if n < NT else n)
                    for k in range(NK):
                        ins = nc.tensor.transpose(bT[u % 2][:, k * P:(k + 1) * P], xn[n % 2][:, k * P:(k + 1) * P], ident[:])
                    ins.then_inc(xt_ps.sem, 1)

                wait(pe, cx_lo, b, 1)
                for g in range(NG):
                    for k in range(NK):
                        ins = product(bM[0][:, g * KEYS:(g + 1) * KEYS], lambda h: wk[h][:, k, g * P:(g + 1) * P],
                                      lambda h: cxt[h][:, k, :], k, NK)
                ins.then_inc(k_ps.sem, 1)
                for k in range(NK):
                    ins = product(bM[1][0:KEYS, :], lambda h: cxt[h][:, k, :], lambda h: wv[h][:, k, :], k, NK)
                ins.then_inc(v_ps.sem, 1)
                for t in range(NT):
                    x_transpose(t)
                wait(pe, x_lo, b, NT)
                for g in range(NG):
                    if g == 0:
                        wait(pe, k_full, b, 1)
                    elif g == 1:
                        wait(pe, v_done, b, 1)
                    else:
                        wait(pe, q_lo, b, g - 1)
                    for k in range(NK):
                        ins = product(bM[g % 2][:], lambda h: wq[h][:, k, g * P:(g + 1) * P], lambda h: xt[h][:, k, :], k, NK)
                    ins.then_inc(q_ps.sem, 1)
                wait(pe, k_lo, b, 1)
                wait(pe, q_lo, b, NG)
                for s in range(SLOTS):
                    if s < STEPS:
                        t, g = s // NG, s % NG
                        if s >= 2:
                            wait(pe, s_copy, b, s - 1)
                        product(bM[s % 2][:, 0:HG * KEYS], lambda h: qt[h][:, g, t * P:(t + 1) * P],
                                lambda h: kb[h][:, g].rearrange("p h n -> p (h n)"), 0, 1).then_inc(s_ps.sem, 1)
                    if 2 <= s < STEPS + 2:
                        i = s - 2
                        wait(pe, p_done, b, i + 1)
                        if i:
                            wait(pe, pt_copy, b, i)
                        for j in range(HG):
                            ins = nc.tensor.transpose(bP[0:KEYS, j * P:(j + 1) * P], pr[i % 2][:, j, :], ident[:])
                        ins.then_inc(pt_ps.sem, 1)
                    if 3 <= s < STEPS + 3:
                        i = s - 3
                        t, g = i // NG, i % NG
                        wait(pe, pt_copy, b, i + 1)
                        if g == 0 and t:
                            wait(pe, o_norm, b, t)
                        for j in range(HG):
                            c = (g * HG + j) * HD0
                            ins = mm(bO[:, c:c + HD0], pt[i % 2][0:KEYS, j, :], v[0:KEYS, c:c + HD0], start=True, stop=True)
                        ins.then_inc(o_ps.sem, 1)
                    if s % 4 == 0 and 0 <= (s - 8) // 4 < NT:
                        t = (s - 8) // 4
                        wait(pe, o_norm, b, t + 1)
                        if t == 0:
                            wait(pe, x_lo, b, NT)
                        else:
                            wait(pe, ao_lo, b, t)
                        for k in range(NK):
                            ins = nc.tensor.transpose(bT[0][:, k * P:(k + 1) * P], ao[:, k * P:(k + 1) * P], ident[:])
                        ins.then_inc(ao_ps.sem, 1)
                    if s % 4 == 1 and 0 <= (s - 9) // 4 < NT:
                        t = (s - 9) // 4
                        wait(pe, ao_lo, b, t + 1)
                        if t:
                            wait(pe, res1, b, t)
                        for k in range(NK):
                            ins = product(bY[:], lambda h: aot[h][:, k, :], lambda h: wo[h][:, k, :], k, NK)
                        ins.then_inc(y_ps.sem, 1)
                    if s % 4 == 0 and 0 <= (s - 12) // 4 < NT:
                        x_transpose(NT + (s - 12) // 4)
                wait(pe, x_lo, b, 2 * NT)
                for m in range(NM + 1):
                    if m < NM:
                        wait(pe, w_lo, b, m + 1)
                        if m >= 2:
                            wait(pe, gelu_done, b, m - 1)
                        for k in range(NK):
                            ins = product(bM[m % 2][:], lambda h: wx[m % NW][h][:, k * P:(k + 1) * P],
                                          lambda h: xt[h][:, k, :], k, NK)
                        ins.then_inc(h_ps.sem, 1)
                    if m:
                        i = m - 1
                        wait(pe, h_lo, b, i + 1)
                        for t in range(NT):
                            ins = product(acc[t][:], lambda h: hx[i % 2][h][:, t * P:(t + 1) * P],
                                          lambda h: wx[i % NW][h][:, D:2 * D], i, NM)
                            if i == NM - 1:
                                ins.then_inc(z_ps.sem, 1)
                        if i < NM - 1:
                            ins.then_inc(m_ps.sem, 1)

        @block.vector
        def _(dve):
            vec = nc.vector
            chain = Chain(dv.sem)
            prime(dve, [cx_lo, k_full, k_lo, v_done, q_lo, x_lo, var_done, xn_done, top_done, p_done, o_norm, ao_lo,
                        res1, res2, w_lo, h_hi, h_lo, dv])
            dve.wait_ge(s_const, 96)
            vec.tensor_scalar(bq[:], bq[:], WS, None, ALU.mult).then_inc(s_bias, 1)
            vec.tensor_scalar(bk[:], bk[:], WS, None, ALU.mult).then_inc(s_bias, 1)
            dve.wait_ge(s_tanh, 1)
            vec.tensor_scalar(gs[:], gt[:], 1 / WS, None, ALU.mult).then_inc(s_bias, 1)
            vec.tensor_scalar(gbo[:], gbo[:], gt[:, 0:1], None, ALU.mult).then_inc(s_bias, 1)
            for n, (_, w) in enumerate(STAGED):
                dve.wait_ge(s_whi, n + 1)
                vec.scalar_tensor_tensor(w[1][:].rearrange("p k n -> p (k n)"), wstage[n % 2][:].rearrange("p k n -> p (k n)"),
                                         WS, w[0][:].rearrange("p k n -> p (k n)"), ALU.mult, ALU.subtract).then_inc(s_wlo, 1)
            dve.wait_ge(s_bias, 4)
            dve.wait_ge(s_setup, 1)
            with dve.Fori(0, B) as b:
                chain.n = 0

                def after(n):
                    wait(dve, dv, b, n)

                def hold(s_, n):
                    wait(dve, s_, b, n)
                    dve.nop(nofuse=True)

                def stats(n, src):
                    i = chain.add(vec.bn_stats(stat[:, n, :], src))
                    hold(dv, i)
                    i = chain.add(vec.bn_aggr(mean[:, n, :], stat[:, n, :]))
                    after(i)
                    vec.tensor_scalar(vare[:, n:n + 1], mean[:, n, 1:2], EPS, None, ALU.add).then_inc(var_done.sem, 1)

                def normalise(n, src):
                    wait(dve, rstd_done, b, n + 1)
                    if n >= 2:
                        wait(dve, xt_ps, b, n - 1)
                    vec.tensor_scalar(xn[n % 2][:], src, mean[:, n, 0:1], rstd[:, n:n + 1], ALU.subtract, ALU.mult)\
                        .then_inc(xn_done.sem, 1)

                def x_low(n):
                    t, u = n % NT, (1 + n if n < NT else 1)
                    wait(dve, x_hi, b, n + 1)
                    vec.tensor_tensor(xt[1][:, :, t * P:(t + 1) * P], bT[u % 2][:].rearrange("p (k n) -> p k n", k=NK),
                                      xt[0][:, :, t * P:(t + 1) * P], ALU.subtract).then_inc(x_lo.sem, 1)

                dve.wait_ge(ld_x, b * 16 + 16)
                for t in range(NT):
                    stats(t, xin[:, t, :])
                wait(dve, cx_hi, b, 1)
                vec.tensor_tensor(cxt[1][:], bT[0][:, 0:NK * KEYS].rearrange("p (k n) -> p k n", k=NK), cxt[0][:], ALU.subtract)\
                    .then_inc(cx_lo.sem, 1)
                for t in range(2):
                    normalise(t, xin[:, t, :])
                wait(dve, k_ps, b, 1)
                vec.tensor_tensor(kf[:], bM[0][:, 0:NG * KEYS].rearrange("p (g n) -> p g n", g=NG),
                                  bk[:].unsqueeze(2).to_broadcast([P, NG, KEYS]), ALU.add).then_inc(k_full.sem, 1)
                wait(dve, v_ps, b, 1)
                vec.scalar_tensor_tensor(v[0:KEYS, :], bM[1][0:KEYS, :], 1 / WS, bv[0:KEYS, :], ALU.mult, ALU.add)\
                    .then_inc(v_done.sem, 1)
                wait(dve, k_hi, b, 1)
                for j in range(HG):
                    r = slice(j * HD0, (j + 1) * HD0)
                    ins = vec.tensor_tensor(kb[1][r, :, j, :], kf[r, :, :], kb[0][r, :, j, :], ALU.subtract)
                ins.then_inc(k_lo.sem, 1)
                for t in range(NT):
                    if t >= 2:
                        normalise(t, xin[:, t, :])
                    x_low(t)
                for g in range(NG):
                    wait(dve, q_hi, b, g + 1)
                    vec.scalar_tensor_tensor(qt[1][:, g, :], bM[g % 2][:], bq[:, g:g + 1], qt[0][:, g, :], ALU.add,
                                             ALU.subtract).then_inc(q_lo.sem, 1)
                for s in range(SLOTS):
                    if s < STEPS:
                        hold(s_copy, s + 1)
                        if s >= 3:
                            hold(p_done, s - 2)
                        for j in range(HG):
                            ins = vec.max(top1[s % 3][:, j, :], sc[s % 3][:, j, :])
                        hold(dv, chain.add(ins))
                        for j in range(HG):
                            ins = vec.match_replace(rep[:, j, :], top1[s % 3][:, j, :], sc[s % 3][:, j, :], LOWEST)
                        hold(dv, chain.add(ins))
                        for j in range(HG):
                            ins = vec.max(top2[s % 3][:, j, :], rep[:, j, :])
                        ins.then_inc(top_done.sem, 1)
                    if 1 <= s <= STEPS:
                        i = s - 1
                        t, g = i // NG, i % NG
                        wait(dve, e_done, b, i + 1)
                        wait(dve, top_done, b, i + 1)
                        if i >= 2:
                            wait(dve, pt_ps, b, i - 1)
                        for j in range(HG):
                            h = g * HG + j
                            ins = vec.scalar_tensor_tensor(pr[i % 2][:, j, :], sc[i % 3][:, j, :],
                                                           top2[i % 3][:, j, TOP - 9:TOP - 8], ex[i % 2][:, j, :],
                                                           ALU.is_ge, ALU.mult, accum_out=rsum[:, t, h:h + 1])
                        ins.then_inc(p_done.sem, 1)
                    if s % 4 == 3 and 0 <= (s - 7) // 4 < NT:
                        t = (s - 7) // 4
                        wait(dve, p_done, b, NG * (t + 1))
                        i = chain.add(vec.reciprocal(rinv[:, t, :], rsum[:, t, :]))
                        after(i)
                        wait(dve, o_ps, b, NG * (t + 1))
                        if t:
                            wait(dve, ao_ps, b, t)
                        vec.tensor_tensor(ao[:].rearrange("p (h d) -> p h d", h=H), bO[:].rearrange("p (h d) -> p h d", h=H),
                                          rinv[:, t, :].unsqueeze(2).to_broadcast([P, H, HD0]), ALU.mult)\
                            .then_inc(o_norm.sem, 1)
                    if s % 4 == 0 and 0 <= (s - 8) // 4 < NT:
                        t = (s - 8) // 4
                        wait(dve, ao_hi, b, t + 1)
                        vec.tensor_tensor(aot[1][:], bT[0][:].rearrange("p (k n) -> p k n", k=NK), aot[0][:],
                                          ALU.subtract).then_inc(ao_lo.sem, 1)
                    if s % 4 == 2 and 0 <= (s - 10) // 4 < NT:
                        t = (s - 10) // 4
                        wait(dve, y_ps, b, t + 1)
                        wait(dve, xa_done, b, 1)
                        if t == 0:
                            dve.wait_ge(x_out.sem, b * 16 + 1)
                        vec.scalar_tensor_tensor(xr[:, t, :], bY[:], gs[:, 0:1], xa[:, t, :], ALU.mult, ALU.add)\
                            .then_inc(res1.sem, 1)
                        wait(dve, res1, b, t + 1)
                        stats(NT + t, xr[:, t, :])
                    if s % 4 == 3 and 0 <= (s - 11) // 4 < NT:
                        t = (s - 11) // 4
                        normalise(NT + t, xr[:, t, :])
                    if s % 4 == 1 and 0 <= (s - 13) // 4 < NT:
                        x_low(NT + (s - 13) // 4)

                def w_low(m):
                    wait(dve, w_hi, b, m + 1)
                    vec.scalar_tensor_tensor(wx[m % NW][1][:], wr[m % 2][:], WS, wx[m % NW][0][:], ALU.mult, ALU.subtract)\
                        .then_inc(w_lo.sem, 1)

                w_low(0)
                w_low(1)
                for m in range(NM):
                    wait(dve, gelu_done, b, m + 1)
                    if m >= 2:
                        wait(dve, m_ps, b, m - 1)
                    vec.tensor_copy(hx[m % 2][0][:], hf[m % 2][:]).then_inc(h_hi.sem, 1)
                    wait(dve, h_hi, b, m + 1)
                    vec.tensor_tensor(hx[m % 2][1][:], hf[m % 2][:], hx[m % 2][0][:], ALU.subtract).then_inc(h_lo.sem, 1)
                    if m + 2 < NM:
                        w_low(m + 2)
                wait(dve, xa_done, b, 2)
                for t in range(NT):
                    wait(dve, z_ps, b, t + 1)
                    vec.scalar_tensor_tensor(xr[:, t, :], acc[t][:], gs[:, 2:3], xa[:, t, :], ALU.mult, ALU.add)\
                        .then_inc(res2.sem, 1)
            assert chain.n == DVE_LINKS, chain.n


def layer1(nc, io):
    DVE_LINKS = 32
    with ExitStack() as ctx:
        sb = lambda name, shape, dt=F32: ctx.enter_context(nc.sbuf_tensor("l1_" + name, shape, dt))
        pb = lambda name, dt=F32: ctx.enter_context(nc.psum_tensor("l1_" + name, [P, 512], dt))
        sem = lambda name: ctx.enter_context(nc.semaphore("l1_" + name))
        sig = lambda name, per: Signal(nc, ctx, "l1_" + name, per)
        pair = lambda name, shape: [sb(name + h, shape, F16) for h in "hl"]

        kvw = pair("kvw", [P, NK, KVC])
        qdw = pair("qdw", [P, NK, QC])
        quw = pair("quw", [P, 2, 4, 512])
        kuw = pair("kuw", [P, H * HD])
        krw = pair("krw", [P, R])
        vuw = pair("vuw", [P, H * HD])
        ow = pair("ow", [P, 2 * NK, D])
        fcw = sb("fcw", [P, NK, F], F16)
        prw = sb("prw", [P, NM, D], F16)
        lru = sb("lru", [P, F], F16)
        lrz = sb("lrz", [P, S], F16)
        vw = pair("vw", [P, NK, RANK])
        fbw = sb("fbw", [RANK, RANK])
        fsc = sb("fsc", [P, NM])
        gsc = sb("gsc", [P, D])
        gs = sb("gs", [P, 4])
        ident = sb("ident", [P, P])
        half = sb("half", [P, 1])
        keyno = sb("keyno", [P, KEYS])
        trig = sb("trig", [P, NT, 2, R // 2])
        ktrig = sb("ktrig", [P, 2, R // 2])

        xin = sb("xin", [P, NT, D])
        xr = sb("xr", [P, NT, D])
        xo = sb("xo", [P, NT, D])
        xn = [sb(f"xn{i}", [P, D]) for i in range(2)]
        stat = sb("stat", [P, 8, 6])
        mean = sb("mean", [P, 8, 2])
        vare = sb("vare", [P, 8])
        rstd = sb("rstd", [P, 8])
        xt = pair("xt", [P, NK, S])
        cx = sb("cx", [P, D])
        cxt = pair("cxt", [P, NK, KEYS])
        kvt = pair("kvt", [P, KEYS])
        krm = sb("krm", [P, 2, 2, R // 2])
        kr = sb("kr", [P, R])
        kc = pair("kc", [P, H, KEYS])
        vc = sb("vc", [P, H * HD])
        qct = pair("qct", [P, 2, S])
        qk = sb("qk", [P, H, P])
        rm = [sb(f"rm{i}", [P, 8, 2, R // 2]) for i in range(2)]
        qkt = pair("qkt", [P, H, P])
        segi = sb("segi", [P, NT], I32)
        segf = sb("segf", [P, NT])
        okay = sb("okay", [P, NT, KEYS])
        pen = sb("pen", [P, NT, KEYS])
        sc = [sb(f"sc{i}", [P, HG, KEYS]) for i in range(2)]
        ex = [sb(f"ex{i}", [P, HG, KEYS]) for i in range(3)]
        smax = sb("smax", [P, 2, HG])
        rsum = sb("rsum", [P, NT, H])
        rinv = sb("rinv", [P, NT, H])
        pt = [sb(f"pt{i}", [P, HG, P]) for i in range(2)]
        ao = sb("ao", [P, 2 * D])
        aot = pair("aot", [P, 2 * NK, P])
        rl = [sb(f"rl{i}", [P, S]) for i in range(2)]
        hf = [sb(f"hf{i}", [P, S]) for i in range(2)]
        hx = [pair(f"hx{i}", [P, S]) for i in range(2)]
        zf = sb("zf", [RANK, S])

        bT = [pb("bT0"), pb("bT1")]
        bS, bW = pb("bS"), pb("bW")
        bP, bU, bO, bY = pb("bP"), pb("bU"), pb("bO"), pb("bY")
        bM = [bS, bW]
        acc = [bP, bU, bO, bY]
        x_v = io["mid"].rearrange("b (t p) d -> b p t d", p=P)
        out_v = io["out"].rearrange("b (t p) d -> b p t d", p=P)

        with ExitStack() as sctx:
            ssem = lambda name: sctx.enter_context(nc.semaphore("l1s_" + name))
            stage = [xo[:].rearrange("p t n -> p (t n)"), xr[:].rearrange("p t n -> p (t n)")]
            rounded = qk[:].rearrange("p h n -> p (h n)")
            tern = ao[:].bitcast(F16)
            small = sctx.enter_context(nc.sbuf_tensor("l1s_small", [P, 512], F32))
            gates, gt, gate = small[:, 0:4], small[:, 4:8], small[:, 8:9]
            asum, scale, inv = small[:, 16:36], small[:, 48:68], small[:, 80:100]
            vraw = small[:, 128:128 + NK * RANK]
            diag = rl[0][:, 0:P]
            ones = rl[0][:, P:2 * P]
            u = hf[0][:, 0:NM * RANK].rearrange("p (m r) -> p m r", m=NM)
            us = hf[1][:, 0:NM * RANK].rearrange("p (m r) -> p m r", m=NM)
            ident16 = rl[1][:].bitcast(F16)[:, 0:P]

            flat = lambda w, h: w[h][:]
            SPLIT = [
                (io["L1_xattn_w_kv_comp"], P, NK * KVC, [flat(kvw, h).rearrange("p k n -> p (k n)") for h in (0, 1)]),
                (io["L1_xattn_w_q_down"], P, NK * QC, [flat(qdw, h).rearrange("p k n -> p (k n)") for h in (0, 1)]),
                (io["quw"][0:P], P, 2048, [flat(quw, h)[:, 0].rearrange("p u n -> p (u n)") for h in (0, 1)]),
                (io["quw"][P:QC], QR, 2048, [flat(quw, h)[0:QR, 1].rearrange("p u n -> p (u n)") for h in (0, 1)]),
                (io["L1_xattn_w_k_up"], P, H * HD, [flat(kuw, h) for h in (0, 1)]),
                (io["L1_xattn_w_k_rope"], P, R, [flat(krw, h) for h in (0, 1)]),
                (io["L1_xattn_w_v_up"], P, H * HD, [flat(vuw, h) for h in (0, 1)]),
                (io["wout"][:, 0:2048], P, 2048, [flat(ow, h)[:, 0:NK].rearrange("p k n -> p (k n)") for h in (0, 1)]),
                (io["wout"][:, 2048:4096], P, 2048, [flat(ow, h)[:, NK:2 * NK].rearrange("p k n -> p (k n)") for h in (0, 1)]),
            ]
            NS = len(SPLIT)
            NTERN = 8
            s_const, s_c2 = ssem("const"), ssem("c2")
            s_ld = [ssem("ld0"), ssem("ld1")]
            s_hi, s_lo = ssem("hi"), ssem("lo")
            s_abs, s_scale, s_round, s_clip = ssem("abs"), ssem("scale"), ssem("round"), ssem("clip")
            s_tern, s_tps, s_tev = ssem("tern"), ssem("tps"), ssem("tev")
            s_id, s_tanh, s_small, s_us = ssem("id"), ssem("tanh"), ssem("small"), ssem("us")
            s_ups, s_uhi, s_ulo = ssem("ups"), ssem("uhi"), ssem("ulo")
            s_diag, s_gps, s_g = ssem("diag"), ssem("gps"), ssem("g")
            block = sctx.enter_context(nc.Block())

            @block.sync
            def _(sp):
                for n in range(NS + NTERN):
                    if n >= 2:
                        if n - 2 < NS:
                            sp.wait_ge(s_lo, n - 1)
                        else:
                            sp.wait_ge(s_round, n - 1 - NS)
                    if n < NS:
                        src, rows, cols, _ = SPLIT[n]
                        if n < 2:
                            dst = stage[n][:, 0:cols].rearrange("p (k n) -> p k n", k=NK)
                            src = src.rearrange("(k p) n -> p k n", p=P)
                        else:
                            dst = stage[n % 2][0:rows, 0:cols]
                        sp.dma_start(dst, src).then_inc(s_ld[n % 2], 16)
                    else:
                        c = n - NS
                        if c < 4:
                            src = io["L1_ffn_w_fc"][c * 4 * P:(c + 1) * 4 * P, :].rearrange("(m p) n -> p m n", p=P)
                            sp.dma_start(stage[n % 2].rearrange("p (m n) -> p m n", m=4), src).then_inc(s_ld[n % 2], 16)
                        else:
                            c -= 4
                            sp.dma_start(stage[n % 2], io["L1_ffn_w_proj"][c * P:(c + 1) * P, :]).then_inc(s_ld[n % 2], 16)

            @block.gpsimd
            def _(pool):
                for dst, src in ((gates[:, 0:2], io["g_xattn"]), (gates[:, 2:4], io["g_ffn"]), (gate, io["L1_ffn_gate"])):
                    pool.dma_start(dst, src.partition_broadcast(P)).then_inc(s_const, 16)
                pool.dma_start(trig[:], io["trig"]).then_inc(s_const, 16)
                pool.dma_start(ktrig[0:KEYS], io["ktrig"]).then_inc(s_const, 16)
                pool.dma_start(vraw, io["vt"]).then_inc(s_const, 16)
                pool.dma_start(u, io["u"]).then_inc(s_const, 16)
                pool.dma_start(fbw[:], io["fbt"]).then_inc(s_const, 16)
                nc.gpsimd.memset(ident[:], 0.0).then_inc(s_c2, 1)
                nc.gpsimd.memset(half[:], -0.5).then_inc(s_id, 1)
                nc.gpsimd.memset(ones, 1.0).then_inc(s_id, 1)
                nc.gpsimd.memset(lru[:], 0.0).then_inc(s_id, 1)
                nc.gpsimd.memset(lrz[:], 0.0).then_inc(s_id, 1)
                nc.gpsimd.iota(keyno[:], [[1, KEYS]], base=0, channel_multiplier=0,
                               allow_small_or_imprecise_dtypes=True).then_inc(s_id, 1)
                pool.wait_ge(s_c2, 1)
                nc.gpsimd.affine_select(out=ident[:], in_=ident[:], compare_op=ALU.not_equal, fill=1.0, base=0,
                                        pattern=[[-1, P]], channel_multiplier=1).then_inc(s_id, 1)

            @block.scalar
            def _(act):
                act.wait_ge(s_const, 128)
                nc.scalar.activation(gt, gates, ACT.Tanh).then_inc(s_tanh, 1)
                nc.scalar.activation(vw[0][:].rearrange("p k r -> p (k r)"), vraw, ACT.Copy, scale=WS).then_inc(s_tanh, 1)
                for n, (_, rows, cols, dst) in enumerate(SPLIT):
                    act.wait_ge(s_ld[n % 2], 16 * (n // 2 + 1))
                    nc.scalar.activation(dst[0], stage[n % 2][0:rows, 0:cols], ACT.Copy, scale=WS).then_inc(s_hi, 1)

                def shift_back(c):
                    act.wait_ge(s_clip, c + 1)
                    if c:
                        act.wait_ge(s_tps, 4 * c)
                    nc.scalar.activation(tern, rounded, ACT.Copy, bias=-ROUND).then_inc(s_tern, 1)
                    for q in range(4):
                        act.wait_ge(s_tps, 4 * c + q + 1)
                        src = bM[q % 2][:].bitcast(F16)[:, 0:512].rearrange("p (k n) -> p k n", k=4)
                        dst = fcw[:, :, (4 * c + q) * P:(4 * c + q + 1) * P] if c < 4 else \
                            prw[:, 4 * q:4 * q + 4, (c - 4) * P:(c - 3) * P]
                        nc.scalar.activation(dst, src, ACT.Copy).then_inc(s_tev, 1)

                for c in range(NTERN):
                    n = NS + c
                    act.wait_ge(s_ld[n % 2], 16 * (n // 2 + 1))
                    rows = 4 if c < 4 else 1
                    w = 2048 // rows
                    for q in range(rows):
                        i = 4 * c + q if c < 4 else 12 + c
                        ins = nc.scalar.activation(pt[q % 2][:].rearrange("p h n -> p (h n)") if w == 512 else
                                                   qkt[0][:].rearrange("p h n -> p (h n)"),
                                                   stage[n % 2][:, q * w:(q + 1) * w], ACT.Abs, accum_out=asum[:, i:i + 1])
                        ins.then_inc(s_abs, 1)
                        if q < rows - 1 or c:
                            act.wait_ge(s_abs, min(4 * c, 16) + max(c - 4, 0) + q + 1)
                    if c:
                        shift_back(c - 1)
                shift_back(NTERN - 1)
                for q in range(4):
                    act.wait_ge(s_ups, q + 1)
                    cols = slice(q * 512, (q + 1) * 512)
                    nc.scalar.activation(lru[0:RANK, cols], bM[q % 2][0:RANK, :], ACT.Copy).then_inc(s_uhi, 1)
                    nc.scalar.activation(lru[64:64 + RANK, cols], bM[q % 2][0:RANK, :], ACT.Copy).then_inc(s_uhi, 1)

            @block.vector
            def _(dve):
                vec = nc.vector
                dve.wait_ge(s_id, 6)
                vec.tensor_copy(ident16, ident[:]).then_inc(s_small, 1)
                dve.wait_ge(s_tanh, 2)
                vec.tensor_scalar(gs[:], gt, 1 / WS, None, ALU.mult).then_inc(s_small, 1)
                vec.scalar_tensor_tensor(vw[1][:].rearrange("p k r -> p (k r)"), vraw, WS, vw[0][:].rearrange("p k r -> p (k r)"),
                                         ALU.mult, ALU.subtract).then_inc(s_small, 1)
                for n, (_, rows, cols, dst) in enumerate(SPLIT):
                    dve.wait_ge(s_hi, n + 1)
                    vec.scalar_tensor_tensor(dst[1], stage[n % 2][0:rows, 0:cols], WS, dst[0], ALU.mult, ALU.subtract)\
                        .then_inc(s_lo, 1)
                for c in range(NTERN):
                    rows = 4 if c < 4 else 1
                    w = 2048 // rows
                    i = 4 * c if c < 4 else 12 + c
                    cols = slice(i, i + rows)
                    dve.wait_ge(s_abs, i + rows)
                    vec.tensor_scalar(scale[:, cols], asum[:, cols], 1 / w, 1e-5, ALU.mult, ALU.max).then_inc(s_scale, 1)
                    dve.wait_ge(s_scale, 2 * c + 1)
                    vec.reciprocal(inv[:, cols], scale[:, cols]).then_inc(s_scale, 1)
                    dve.wait_ge(s_scale, 2 * c + 2)
                    if c:
                        dve.wait_ge(s_tern, c)
                    for q in range(rows):
                        ins = vec.tensor_scalar(rounded[:, q * w:(q + 1) * w], stage[(NS + c) % 2][:, q * w:(q + 1) * w],
                                                inv[:, i + q:i + q + 1], ROUND, ALU.mult, ALU.add)
                    ins.then_inc(s_round, 1)
                    dve.wait_ge(s_round, c + 1)
                    vec.tensor_scalar(rounded, rounded, ROUND + 1, ROUND - 1, ALU.min, ALU.max).then_inc(s_clip, 1)
                vec.tensor_copy(fsc[:], scale[:, 0:NM]).then_inc(s_small, 1)
                vec.tensor_tensor(us, u, inv[:, 0:NM].unsqueeze(2).to_broadcast([P, NM, RANK]), ALU.mult).then_inc(s_us, 1)
                dve.wait_ge(s_us, 1)
                vec.tensor_scalar(us, us, gate, None, ALU.mult).then_inc(s_us, 1)
                for j in range(4):
                    if j:
                        dve.wait_ge(s_gps, j)
                    vec.tensor_scalar(diag, ident[:], scale[:, 16 + j:17 + j], None, ALU.mult).then_inc(s_diag, 1)
                for q in range(4):
                    dve.wait_ge(s_uhi, 2 * q + 2)
                    cols = slice(q * 512, (q + 1) * 512)
                    vec.tensor_tensor(lru[32:32 + RANK, cols], bM[q % 2][0:RANK, :], lru[0:RANK, cols], ALU.subtract)\
                        .then_inc(s_ulo, 1)
                dve.wait_ge(s_gps, 4)
                vec.tensor_scalar(gsc[:], bT[0][:], gt[:, 3:4], None, ALU.mult).then_inc(s_g, 1)

            @block.tensor
            def _(pe):
                pe.wait_ge(s_small, 1)
                for c in range(NTERN):
                    pe.wait_ge(s_tern, c + 1)
                    for q in range(4):
                        n = 4 * c + q
                        if n >= 2:
                            pe.wait_ge(s_tev, n - 1)
                        for k in range(4):
                            ins = nc.tensor.transpose(bM[q % 2][:].bitcast(F16)[:, k * P:(k + 1) * P],
                                                      tern[:, (4 * q + k) * P:(4 * q + k + 1) * P], ident16)
                        ins.then_inc(s_tps, 1)
                pe.wait_ge(s_us, 2)
                pe.wait_ge(s_tev, 4 * NTERN)
                for j in range(4):
                    pe.wait_ge(s_diag, j + 1)
                    nc.tensor.matmul(bT[0][:, j * P:(j + 1) * P], ones, diag, start=True, stop=True).then_inc(s_gps, 1)
                for q in range(4):
                    if q >= 2:
                        pe.wait_ge(s_ulo, q - 1)
                    for k in range(4):
                        ins = nc.tensor.transpose(bM[q % 2][0:RANK, k * P:(k + 1) * P], us[:, 4 * q + k, :], ident[:])
                    ins.then_inc(s_ups, 1)

        ld_x, ld_c, ld_s = sem("ld_x"), sem("ld_c"), sem("ld_s")
        cxt_ps, kv_ps, kr_ps, v_ps, kn_ps, krt_ps = (sig("cxt_ps", 1), sig("kv_ps", 1), sig("kr_ps", 1), sig("v_ps", 2),
                                                     sig("kn_ps", NG), sig("krt_ps", 1))
        xt_ps, qc_ps, u_ps, qt_ps = sig("xt_ps", 2 * NT), sig("qc_ps", 2), sig("u_ps", STEPS), sig("qt_ps", STEPS)
        s_ps, pt_ps, o_ps, ao_ps, y_ps = (sig("s_ps", STEPS), sig("pt_ps", STEPS), sig("o_ps", STEPS), sig("ao_ps", 2 * NT),
                                          sig("y_ps", NT))
        z1_ps, z2_ps, h_ps, m_ps, z_ps = sig("z1_ps", 1), sig("z2_ps", 1), sig("h_ps", NM), sig("m_ps", NM - 1), sig("z_ps", NT)
        cx_hi, kv_hi, kn_hi, kr_hi, v_copy = (sig("cx_hi", 1), sig("kv_hi", 1), sig("kn_hi", NG), sig("kr_hi", 1),
                                              sig("v_copy", 2))
        x_hi, qc_hi, nope, qt_hi = sig("x_hi", 2 * NT), sig("qc_hi", 2), sig("nope", 2 * NT), sig("qt_hi", STEPS)
        e_done, pt_copy, ao_hi, z_hi = sig("e_done", STEPS), sig("pt_copy", STEPS), sig("ao_hi", 2 * NT), sig("z_hi", 1)
        relu_done, sq_done = sig("relu_done", NM), sig("sq_done", NM)
        cx_lo, kv_lo, kn_lo, kr_lo, kr_rope = (sig("cx_lo", 1), sig("kv_lo", 1), sig("kn_lo", NG), sig("kr_lo", 1),
                                               sig("kr_rope", 1))
        x_lo, var_done, xn_done, qc_lo = sig("x_lo", 2 * NT), sig("var_done", 2 * NT), sig("xn_done", 2 * NT), sig("qc_lo", 2)
        rot, qt_lo, masked, top_done, sum_done = (sig("rot", 2 * NT), sig("qt_lo", STEPS), sig("masked", STEPS),
                                                  sig("top_done", STEPS), sig("sum_done", STEPS))
        o_norm, ao_lo, res1 = sig("o_norm", NT), sig("ao_lo", 2 * NT), sig("res1", NT)
        z_copy, z_lo, h_hi, h_lo, y_sc = sig("z_copy", 1), sig("z_lo", 1), sig("h_hi", NM), sig("h_lo", NM), sig("y_sc", NT)
        dv = sig("dv", DVE_LINKS)
        rstd_done, spread, shifted, roped, res2 = (sig("rstd_done", 2 * NT), sig("spread", 1), sig("shifted", STEPS),
                                                   sig("roped", 2 * NT), sig("res2", NT))
        x_out = sig("x_out", 16)

        block = ctx.enter_context(nc.Block())
        S2 = SLOTS + 1
        bcast = lambda ap, n: ap.unsqueeze(1).to_broadcast([ap.shape[0], n, ap.shape[-1]])

        @block.sync
        def _(sp):
            with sp.Fori(0, B) as b:
                wait(sp, res1, b, 0)
                sp.dma_start(xin[:], x_v[b]).then_inc(ld_x, 16)
                sp.dma_start(cx[0:KEYS, :], io["ctx_1024"][b]).then_inc(ld_c, 16)
                sp.dma_start(segi[:], io["seg"][b]).then_inc(ld_s, 16)
                wait(sp, res2, b, NT)
                sp.dma_start(out_v[b], xo[:]).then_inc(x_out.sem, 16)
            sp.wait_ge(x_out.sem, B * 16 + 1)

        @block.gpsimd
        def _(pool):
            prime(pool, [rstd_done, spread, shifted, roped, res2, x_out])
            with pool.Fori(0, B) as b:
                def power(n):
                    wait(pool, var_done, b, n + 1)
                    nc.gpsimd.tensor_tensor(rstd[:, n:n + 1], vare[:, n:n + 1], half[:], ALU.pow).then_inc(rstd_done.sem, 1)

                for t in range(NT):
                    power(t)
                wait(pool, kr_lo, b, 1)
                pool.nop(nofuse=True)
                for h in range(2):
                    ins = nc.gpsimd.tensor_copy(kc[h][HD:P, 1:H, :], kc[h][HD:P, 0:1, :].to_broadcast([R, H - 1, KEYS]))
                ins.then_inc(spread.sem, 1)
                wait(pool, spread, b, 1)

                def rotate(n):
                    wait(pool, rot, b, n + 1)
                    if n >= 2:
                        wait(pool, qt_ps, b, 4 * (n // 2) - (2 if n % 2 == 0 else 0))
                    h = slice(8 * (n % 2), 8 * (n % 2) + 8)
                    c, s = rm
                    nc.gpsimd.tensor_tensor(qk[:, h, HD:HD + R // 2], c[:, :, 0, :], s[:, :, 1, :], ALU.subtract)
                    nc.gpsimd.tensor_tensor(qk[:, h, HD + R // 2:P], s[:, :, 0, :], c[:, :, 1, :], ALU.add)\
                        .then_inc(roped.sem, 1)

                rotate(0)
                rotate(1)
                for s in range(S2):
                    if s < STEPS:
                        wait(pool, top_done, b, s + 1)
                        if s >= 3:
                            wait(pool, sum_done, b, s - 2)
                            wait(pool, pt_ps, b, s - 2)
                        nc.gpsimd.tensor_tensor(ex[s % 3][:], sc[s % 2][:],
                                                smax[:, s % 2, :].unsqueeze(2).to_broadcast([P, HG, KEYS]), ALU.subtract)\
                            .then_inc(shifted.sem, 1)
                    if s % 2 == 1 and s < STEPS - NG:
                        rotate(2 + s // 2)
                    if s % 4 == 3 and 0 <= (s - 11) // 4 < NT:
                        power(NT + (s - 11) // 4)
                for t in range(NT):
                    wait(pool, y_sc, b, t + 1)
                    nc.gpsimd.tensor_tensor(xo[:, t, :], xo[:, t, :], xr[:, t, :], ALU.add).then_inc(res2.sem, 1)

        @block.scalar
        def _(act):
            prime(act, [cx_hi, kv_hi, kn_hi, kr_hi, v_copy, x_hi, qc_hi, nope, qt_hi, e_done, pt_copy, ao_hi, z_hi,
                        relu_done, sq_done])
            four = lambda ap: ap.rearrange("p (k n) -> p k n", k=4)
            with act.Fori(0, B) as b:
                wait(act, cxt_ps, b, 1)
                nc.scalar.activation(cxt[0][:], four(bT[0][:, 0:NK * KEYS]), ACT.Copy).then_inc(cx_hi.sem, 1)

                def x_high(n):
                    wait(act, xt_ps, b, n + 1)
                    t, u = n % NT, (1 + n if n < NT else 1)
                    nc.scalar.activation(xt[0][:, :, t * P:(t + 1) * P], four(bT[u % 2][:]), ACT.Copy).then_inc(x_hi.sem, 1)

                wait(act, kv_ps, b, 1)
                nc.scalar.activation(kvt[0][:], bS[:, 0:KEYS], ACT.Copy, scale=1 / WS).then_inc(kv_hi.sem, 1)
                for t in range(NT):
                    x_high(t)
                for n, bank in enumerate((bO, bY)):
                    wait(act, v_ps, b, n + 1)
                    nc.scalar.activation(vc[0:KEYS, n * 512:(n + 1) * 512], bank[0:KEYS, :], ACT.Copy, scale=1 / WS)\
                        .then_inc(v_copy.sem, 1)
                for g in range(NG):
                    wait(act, kn_ps, b, g + 1)
                    nc.scalar.activation(kc[0][0:HD, g * HG:(g + 1) * HG, :], four(bM[(g + 1) % 2][0:HD, 0:HG * KEYS]), ACT.Copy)\
                        .then_inc(kn_hi.sem, 1)
                wait(act, krt_ps, b, 1)
                nc.scalar.activation(kc[0][HD:P, 0, :], bU[0:R, 0:KEYS], ACT.Copy).then_inc(kr_hi.sem, 1)
                for n, rows in enumerate((P, QR)):
                    wait(act, qc_ps, b, n + 1)
                    nc.scalar.activation(qct[0][0:rows, n, :], bM[n][0:rows, :], ACT.Copy, scale=1 / WS).then_inc(qc_hi.sem, 1)

                def nope_copy(n):
                    wait(act, u_ps, b, 2 * n + 1)
                    if n >= 2:
                        wait(act, qt_ps, b, 4 * (n // 2) - (2 if n % 2 == 0 else 0))
                    nc.scalar.activation(qk[:, 8 * (n % 2):8 * (n % 2) + 8, 0:HD], bU[:].rearrange("p (h n) -> p h n", h=8),
                                         ACT.Copy).then_inc(nope.sem, 1)

                def q_high(n):
                    wait(act, qt_ps, b, n + 1)
                    if n >= NG:
                        wait(act, s_ps, b, n - NG + 1)
                    g = n % NG
                    nc.scalar.activation(qkt[0][:, g * HG:(g + 1) * HG, :], four(bT[0][:]), ACT.Copy).then_inc(qt_hi.sem, 1)

                nope_copy(0)
                nope_copy(1)
                q_high(0)
                q_high(1)
                for s in range(S2):
                    if s % 2 == 0 and s < STEPS - NG:
                        nope_copy(2 + s // 2)
                    if s + 2 < STEPS:
                        q_high(s + 2)
                    if 1 <= s <= STEPS:
                        wait(act, shifted, b, s)
                        e = ex[(s - 1) % 3]
                        nc.scalar.activation(e[:], e[:], ACT.Exp, scale=EXP1).then_inc(e_done.sem, 1)
                    if 2 <= s < STEPS + 2:
                        i = s - 2
                        wait(act, pt_ps, b, i + 1)
                        if i >= 2:
                            wait(act, o_ps, b, i - 1)
                        nc.scalar.activation(pt[i % 2][0:KEYS], four(bP[0:KEYS, :]), ACT.Copy).then_inc(pt_copy.sem, 1)
                    for n in range(2 * NT):
                        if s == 8 + 4 * (n // 2) + n % 2:
                            wait(act, ao_ps, b, n + 1)
                            if n >= 2:
                                wait(act, y_ps, b, n // 2)
                            nc.scalar.activation(aot[0][:, 4 * (n % 2):4 * (n % 2) + 4, :], four(bT[1][:]), ACT.Copy)\
                                .then_inc(ao_hi.sem, 1)
                    if s % 4 == 2 and 0 <= (s - 14) // 4 < NT:
                        x_high(NT + (s - 14) // 4)
                wait(act, z2_ps, b, 1)
                nc.scalar.activation(lrz[0:RANK, :], bP[0:RANK, :], ACT.Copy)
                nc.scalar.activation(lrz[32:32 + RANK, :], bP[0:RANK, :], ACT.Copy).then_inc(z_hi.sem, 1)
                for m in range(NM):
                    wait(act, h_ps, b, m + 1)
                    nc.scalar.activation(rl[m % 2][:], bM[m % 2][:], ACT.Relu, scale=fsc[:, m:m + 1]).then_inc(relu_done.sem, 1)
                    wait(act, relu_done, b, m + 1)
                    if m >= 2:
                        wait(act, h_lo, b, m - 1)
                    nc.scalar.activation(hf[m % 2][:], rl[m % 2][:], ACT.Square).then_inc(sq_done.sem, 1)

        @block.tensor
        def _(pe):
            prime(pe, [cxt_ps, kv_ps, kr_ps, v_ps, kn_ps, krt_ps, xt_ps, qc_ps, u_ps, qt_ps, s_ps, pt_ps, o_ps, ao_ps, y_ps,
                       z1_ps, z2_ps, h_ps, m_ps, z_ps])
            mm = nc.tensor.matmul

            def product(out, lhs, rhs, k, n):
                mm(out, lhs(0), rhs(0), start=(k == 0), stop=False)
                mm(out, lhs(0), rhs(1), start=False, stop=False)
                return mm(out, lhs(1), rhs(0), start=False, stop=(k == n - 1))

            with pe.Fori(0, B) as b:
                pe.wait_ge(ld_c, b * 16 + 16)
                for k in range(NK):
                    ins = nc.tensor.transpose(bT[0][:, k * KEYS:(k + 1) * KEYS], cx[0:KEYS, k * P:(k + 1) * P],
                                              ident[0:KEYS, 0:KEYS])
                ins.then_inc(cxt_ps.sem, 1)

                def x_transpose(n):
                    u = 1 + n if n < NT else 1
                    wait(pe, xn_done, b, n + 1)
                    if u == 2:
                        wait(pe, cx_lo, b, 1)
                    elif 2 <= n < NT:
                        wait(pe, x_lo, b, n - 1)
                    elif n >= NT:
                        wait(pe, ao_lo, b, min(2 * (n - NT + 2), 2 * NT))
                        wait(pe, x_lo, b, n)
                    for k in range(NK):
                        ins = nc.tensor.transpose(bT[u % 2][:, k * P:(k + 1) * P], xn[n % 2][:, k * P:(k + 1) * P], ident[:])
                    ins.then_inc(xt_ps.sem, 1)

                wait(pe, cx_lo, b, 1)
                for k in range(NK):
                    ins = product(bS[:, 0:KEYS], lambda h: kvw[h][:, k, :], lambda h: cxt[h][:, k, :], k, NK)
                ins.then_inc(kv_ps.sem, 1)
                x_transpose(0)
                x_transpose(1)
                wait(pe, kv_lo, b, 1)
                product(bP[0:KEYS, 0:R], lambda h: kvt[h][:], lambda h: krw[h][:], 0, 1).then_inc(kr_ps.sem, 1)
                for n, bank in enumerate((bO, bY)):
                    product(bank[0:KEYS, :], lambda h: kvt[h][:], lambda h: vuw[h][:, n * 512:(n + 1) * 512], 0, 1)\
                        .then_inc(v_ps.sem, 1)
                x_transpose(2)
                x_transpose(3)
                for g in range(NG):
                    if g >= 2:
                        wait(pe, kn_lo, b, g - 1)
                    for j in range(HG):
                        c = (g * HG + j) * HD
                        ins = product(bM[(g + 1) % 2][0:HD, j * KEYS:(j + 1) * KEYS], lambda h: kuw[h][:, c:c + HD],
                                      lambda h: kvt[h][:], 0, 1)
                    ins.then_inc(kn_ps.sem, 1)
                wait(pe, kr_rope, b, 1)
                pe.nop(nofuse=True)
                nc.tensor.transpose(bU[0:R, 0:KEYS], kr[0:KEYS, :], ident[0:KEYS, 0:KEYS]).then_inc(krt_ps.sem, 1)
                wait(pe, x_lo, b, NT)
                wait(pe, kn_lo, b, NG)
                for n, rows in enumerate((P, QR)):
                    for k in range(NK):
                        ins = product(bM[n][0:rows, :], lambda h: qdw[h][:, k, n * P:n * P + rows], lambda h: xt[h][:, k, :],
                                      k, NK)
                    ins.then_inc(qc_ps.sem, 1)

                def project(n):
                    t, r = n // 4, n % 4
                    if n == 0:
                        wait(pe, kr_lo, b, 1)
                        wait(pe, qc_lo, b, 2)
                    elif n % 2 == 1:
                        wait(pe, nope, b, n // 2 + 1)
                    else:
                        wait(pe, rot, b, n // 2)
                    product(bU[:], lambda h: qct[h][:, 0, t * P:(t + 1) * P], lambda h: quw[h][:, 0, r, :], 0, 2)
                    product(bU[:], lambda h: qct[h][0:QR, 1, t * P:(t + 1) * P], lambda h: quw[h][0:QR, 1, r, :], 1, 2)\
                        .then_inc(u_ps.sem, 1)

                def q_transpose(n):
                    g = n % 4
                    wait(pe, nope, b, n // 2 + 1)
                    wait(pe, roped, b, n // 2 + 1)
                    if n:
                        wait(pe, qt_lo, b, n)
                    for j in range(HG):
                        ins = nc.tensor.transpose(bT[0][:, j * P:(j + 1) * P], qk[:, g * HG + j, :], ident[:])
                    ins.then_inc(qt_ps.sem, 1)

                for n in range(4):
                    project(n)
                q_transpose(0)
                q_transpose(1)
                for s in range(S2):
                    if s < STEPS:
                        t, g = s // NG, s % NG
                        if s + 4 < STEPS:
                            project(s + 4)
                        if s == 0:
                            wait(pe, spread, b, 1)
                        else:
                            wait(pe, masked, b, s)
                        wait(pe, qt_lo, b, s + 1)
                        for j in range(HG):
                            h_ = g * HG + j
                            ins = product(bS[:, j * KEYS:(j + 1) * KEYS], lambda h: qkt[h][:, h_, :], lambda h: kc[h][:, h_, :],
                                          0, 1)
                        ins.then_inc(s_ps.sem, 1)
                        if s + 2 < STEPS:
                            q_transpose(s + 2)
                    if 2 <= s < STEPS + 2:
                        i = s - 2
                        wait(pe, e_done, b, i + 1)
                        if i:
                            wait(pe, pt_copy, b, i)
                        for j in range(HG):
                            ins = nc.tensor.transpose(bP[0:KEYS, j * P:(j + 1) * P], ex[i % 3][:, j, :], ident[:])
                        ins.then_inc(pt_ps.sem, 1)
                    if 3 <= s < STEPS + 3:
                        i = s - 3
                        t, g = i // NG, i % NG
                        wait(pe, pt_copy, b, i + 1)
                        if g == 0:
                            wait(pe, o_norm, b, t)
                            wait(pe, v_copy, b, 2)
                        for j in range(HG):
                            h_ = g * HG + j
                            ins = mm((bO, bY)[h_ // 8][:, (h_ % 8) * HD:(h_ % 8 + 1) * HD], pt[i % 2][0:KEYS, j, :],
                                     vc[0:KEYS, h_ * HD:(h_ + 1) * HD], start=True, stop=True)
                        ins.then_inc(o_ps.sem, 1)
                    for n in range(2 * NT):
                        if s == 8 + 4 * (n // 2) + n % 2:
                            t = n // 2
                            wait(pe, o_norm, b, t + 1)
                            wait(pe, ao_lo, b, n)
                            wait(pe, x_lo, b, NT + max(t - 1, 0))
                            for k in range(4):
                                c = (4 * (n % 2) + k) * P
                                ins = nc.tensor.transpose(bT[1][:, k * P:(k + 1) * P], ao[:, c:c + P], ident[:])
                            ins.then_inc(ao_ps.sem, 1)
                    if s % 4 == 2 and 0 <= (s - 10) // 4 < NT:
                        t = (s - 10) // 4
                        wait(pe, ao_lo, b, 2 * t + 2)
                        if t:
                            wait(pe, res1, b, t)
                        for k in range(2 * NK):
                            ins = product(bW[:], lambda h: aot[h][:, k, :], lambda h: ow[h][:, k, :], k, 2 * NK)
                        ins.then_inc(y_ps.sem, 1)
                    if s % 4 == 1 and 0 <= (s - 13) // 4 < NT:
                        x_transpose(NT + (s - 13) // 4)
                wait(pe, x_lo, b, 2 * NT)
                for k in range(NK):
                    ins = product(bU[0:RANK, :], lambda h: vw[h][:, k, :], lambda h: xt[h][:, k, :], k, NK)
                ins.then_inc(z1_ps.sem, 1)
                for m in range(NM + 1):
                    if m < NM:
                        if m >= 2:
                            wait(pe, relu_done, b, m - 1)
                        for k in range(NK):
                            w = fcw[:, k, m * P:(m + 1) * P]
                            mm(bM[m % 2][:], w, xt[0][:, k, :], start=(k == 0), stop=False)
                            mm(bM[m % 2][:], w, xt[1][:, k, :], start=False, stop=False)
                        if m == 0:
                            wait(pe, z_copy, b, 1)
                            pe.nop(nofuse=True)
                            mm(bP[0:RANK, :], fbw[:], zf[:], start=True, stop=True).then_inc(z2_ps.sem, 1)
                            wait(pe, z_lo, b, 1)
                        mm(bM[m % 2][:], lru[0:ZROWS, m * P:(m + 1) * P], lrz[0:ZROWS, :], start=False, stop=True)\
                            .then_inc(h_ps.sem, 1)
                    if m:
                        i = m - 1
                        wait(pe, h_lo, b, i + 1)
                        for t in range(NT):
                            mm(acc[t][:], hx[i % 2][0][:, t * P:(t + 1) * P], prw[:, i, :], start=(i == 0), stop=False)
                            ins = mm(acc[t][:], hx[i % 2][1][:, t * P:(t + 1) * P], prw[:, i, :], start=False,
                                     stop=(i == NM - 1))
                            if i == NM - 1:
                                ins.then_inc(z_ps.sem, 1)
                        if i < NM - 1:
                            ins.then_inc(m_ps.sem, 1)

        @block.vector
        def _(dve):
            vec = nc.vector
            chain = Chain(dv.sem)
            four = lambda ap: ap.rearrange("p (k n) -> p k n", k=4)
            prime(dve, [cx_lo, kv_lo, kn_lo, kr_lo, kr_rope, x_lo, var_done, xn_done, qc_lo, rot, qt_lo, masked, top_done,
                        sum_done, o_norm, ao_lo, res1, z_copy, z_lo, h_hi, h_lo, y_sc, dv])
            with dve.Fori(0, B) as b:
                chain.n = 0

                def after(n):
                    wait(dve, dv, b, n)

                def hold(s_, n):
                    wait(dve, s_, b, n)
                    dve.nop(nofuse=True)

                def stats(n, src):
                    i = chain.add(vec.bn_stats(stat[:, n, :], src))
                    hold(dv, i)
                    i = chain.add(vec.bn_aggr(mean[:, n, :], stat[:, n, :]))
                    after(i)
                    vec.tensor_scalar(vare[:, n:n + 1], mean[:, n, 1:2], EPS, None, ALU.add).then_inc(var_done.sem, 1)

                def normalise(n, src):
                    wait(dve, rstd_done, b, n + 1)
                    if n >= 2:
                        wait(dve, xt_ps, b, n - 1)
                    vec.tensor_scalar(xn[n % 2][:], src, mean[:, n, 0:1], rstd[:, n:n + 1], ALU.subtract, ALU.mult)\
                        .then_inc(xn_done.sem, 1)

                def x_low(n):
                    t, u = n % NT, (1 + n if n < NT else 1)
                    wait(dve, x_hi, b, n + 1)
                    vec.tensor_tensor(xt[1][:, :, t * P:(t + 1) * P], four(bT[u % 2][:]), xt[0][:, :, t * P:(t + 1) * P],
                                      ALU.subtract).then_inc(x_lo.sem, 1)

                dve.wait_ge(ld_x, b * 16 + 16)
                for t in range(NT):
                    stats(t, xin[:, t, :])
                wait(dve, cx_hi, b, 1)
                vec.tensor_tensor(cxt[1][:], four(bT[0][:, 0:NK * KEYS]), cxt[0][:], ALU.subtract).then_inc(cx_lo.sem, 1)
                for t in range(2):
                    normalise(t, xin[:, t, :])
                wait(dve, kv_hi, b, 1)
                vec.scalar_tensor_tensor(kvt[1][:], bS[:, 0:KEYS], 1 / WS, kvt[0][:], ALU.mult, ALU.subtract)\
                    .then_inc(kv_lo.sem, 1)
                dve.wait_ge(ld_s, b * 16 + 16)
                after(chain.add(vec.tensor_copy(segf[:], segi[:])))
                for t in range(NT):
                    i = chain.add(vec.tensor_scalar(okay[:, t, :], keyno[:], segf[:, t:t + 1], -float(LOOKBACK), ALU.subtract,
                                                    ALU.is_ge))
                after(i)
                for t in range(NT):
                    i = chain.add(vec.scalar_tensor_tensor(pen[:, t, :], keyno[:], segf[:, t:t + 1], okay[:, t, :], ALU.is_le,
                                                           ALU.mult))
                after(i)
                pen_link = chain.add(vec.tensor_scalar(pen[:], pen[:], -1.0, -LOWEST, ALU.add, ALU.mult))
                wait(dve, kr_ps, b, 1)
                for c in range(2):
                    i = chain.add(vec.tensor_tensor(krm[0:KEYS, c], bP[0:KEYS, 0:R].rearrange("p (a n) -> p a n", a=2),
                                                    bcast(ktrig[0:KEYS, c, :], 2), ALU.mult))
                after(i)
                vec.tensor_tensor(kr[0:KEYS, 0:R // 2], krm[0:KEYS, 0, 0], krm[0:KEYS, 1, 1], ALU.subtract)
                vec.tensor_tensor(kr[0:KEYS, R // 2:R], krm[0:KEYS, 1, 0], krm[0:KEYS, 0, 1], ALU.add).then_inc(kr_rope.sem, 1)
                for t in range(NT):
                    x_low(t)
                    if t < 2:
                        normalise(t + 2, xin[:, t + 2, :])
                for g in range(NG):
                    wait(dve, kn_hi, b, g + 1)
                    hs = slice(g * HG, (g + 1) * HG)
                    vec.tensor_tensor(kc[1][0:HD, hs, :], four(bM[(g + 1) % 2][0:HD, 0:HG * KEYS]), kc[0][0:HD, hs, :],
                                      ALU.subtract).then_inc(kn_lo.sem, 1)
                wait(dve, kr_hi, b, 1)
                vec.tensor_tensor(kc[1][HD:P, 0, :], bU[0:R, 0:KEYS], kc[0][HD:P, 0, :], ALU.subtract).then_inc(kr_lo.sem, 1)
                for n, rows in enumerate((P, QR)):
                    wait(dve, qc_hi, b, n + 1)
                    vec.scalar_tensor_tensor(qct[1][0:rows, n, :], bM[n][0:rows, :], 1 / WS, qct[0][0:rows, n, :], ALU.mult,
                                             ALU.subtract).then_inc(qc_lo.sem, 1)

                def rotate(n):
                    wait(dve, u_ps, b, 2 * n + 2)
                    if n:
                        wait(dve, roped, b, n)
                    for c in range(2):
                        ins = vec.tensor_tensor(rm[c][:].rearrange("p h a n -> p (h a) n"), bU[:].rearrange("p (h n) -> p h n", h=16),
                                                bcast(trig[:, n // 2, c, :], 16), ALU.mult)
                    ins.then_inc(rot.sem, 1)

                def q_low(n):
                    wait(dve, qt_hi, b, n + 1)
                    hs = slice((n % NG) * HG, (n % NG + 1) * HG)
                    vec.tensor_tensor(qkt[1][:, hs, :], four(bT[0][:]), qkt[0][:, hs, :], ALU.subtract).then_inc(qt_lo.sem, 1)

                rotate(0)
                rotate(1)
                q_low(0)
                q_low(1)
                for s in range(S2):
                    if s % 4 == 3 and 0 <= (s - 7) // 4 < NT:
                        t = (s - 7) // 4
                        wait(dve, sum_done, b, NG * (t + 1))
                        after(chain.add(vec.reciprocal(rinv[:, t, :], rsum[:, t, :])))
                        wait(dve, o_ps, b, NG * (t + 1))
                        if t:
                            wait(dve, ao_ps, b, 2 * t)
                        for n, bank in enumerate((bO, bY)):
                            ins = vec.tensor_tensor(ao[:, n * 512:(n + 1) * 512].rearrange("p (h d) -> p h d", h=8),
                                                    bank[:].rearrange("p (h d) -> p h d", h=8),
                                                    rinv[:, t, 8 * n:8 * n + 8].unsqueeze(2).to_broadcast([P, 8, HD]), ALU.mult)
                        ins.then_inc(o_norm.sem, 1)
                    if s < STEPS:
                        t = s // NG
                        wait(dve, s_ps, b, s + 1)
                        if s >= 2:
                            wait(dve, shifted, b, s - 1)
                        if s == 0:
                            after(pen_link)
                        vec.tensor_tensor(sc[s % 2][:], four(bS[:, 0:HG * KEYS]), bcast(pen[:, t, :], HG), ALU.add)\
                            .then_inc(masked.sem, 1)
                        wait(dve, masked, b, s + 1)
                        vec.tensor_reduce(smax[:, s % 2, :], sc[s % 2][:], AX_X, ALU.max).then_inc(top_done.sem, 1)
                    if s % 2 == 1 and s < STEPS - NG:
                        rotate(2 + s // 2)
                    if s + 2 < STEPS:
                        q_low(s + 2)
                    if 1 <= s <= STEPS:
                        i = s - 1
                        wait(dve, e_done, b, i + 1)
                        vec.tensor_reduce(rsum[:, i // NG, (i % NG) * HG:(i % NG + 1) * HG], ex[i % 3][:], AX_X, ALU.add)\
                            .then_inc(sum_done.sem, 1)
                    for n in range(2 * NT):
                        if s == 8 + 4 * (n // 2) + n % 2:
                            wait(dve, ao_hi, b, n + 1)
                            ks = slice(4 * (n % 2), 4 * (n % 2) + 4)
                            vec.tensor_tensor(aot[1][:, ks, :], four(bT[1][:]), aot[0][:, ks, :], ALU.subtract)\
                                .then_inc(ao_lo.sem, 1)
                    if s % 4 == 3 and 0 <= (s - 11) // 4 < NT:
                        t = (s - 11) // 4
                        wait(dve, y_ps, b, t + 1)
                        if t == 0:
                            wait(dve, res2, b, 0)
                        vec.scalar_tensor_tensor(xr[:, t, :], bW[:], gs[:, 1:2], xin[:, t, :], ALU.mult, ALU.add)\
                            .then_inc(res1.sem, 1)
                        wait(dve, res1, b, t + 1)
                        stats(NT + t, xr[:, t, :])
                    if s % 4 == 0 and 0 <= (s - 12) // 4 < NT:
                        t = (s - 12) // 4
                        normalise(NT + t, xr[:, t, :])
                    if s % 4 == 2 and 0 <= (s - 14) // 4 < NT:
                        x_low(NT + (s - 14) // 4)
                wait(dve, z1_ps, b, 1)
                vec.tensor_scalar(zf[:], bU[0:RANK, :], 1 / WS, None, ALU.mult).then_inc(z_copy.sem, 1)
                wait(dve, z_hi, b, 1)
                vec.tensor_tensor(lrz[64:64 + RANK, :], bP[0:RANK, :], lrz[0:RANK, :], ALU.subtract).then_inc(z_lo.sem, 1)
                for m in range(NM):
                    wait(dve, sq_done, b, m + 1)
                    if m >= 2:
                        wait(dve, m_ps, b, m - 1)
                    vec.tensor_copy(hx[m % 2][0][:], hf[m % 2][:]).then_inc(h_hi.sem, 1)
                    wait(dve, h_hi, b, m + 1)
                    vec.tensor_tensor(hx[m % 2][1][:], hf[m % 2][:], hx[m % 2][0][:], ALU.subtract).then_inc(h_lo.sem, 1)
                for t in range(NT):
                    wait(dve, z_ps, b, t + 1)
                    if t == 0:
                        dve.wait_ge(x_out.sem, b * 16 + 1)
                    vec.tensor_tensor(xo[:, t, :], acc[t][:], gsc[:], ALU.mult).then_inc(y_sc.sem, 1)
            assert chain.n == DVE_LINKS, chain.n


_INS = ['x', 'ctx_1024', 'g_xattn', 'g_ffn', 'L0_xattn_Wq', 'L0_xattn_bq', 'L0_xattn_Wk', 'L0_xattn_bk',
        'L0_xattn_Wv', 'L0_xattn_bv', 'L0_xattn_Wo', 'L0_xattn_bo', 'w12', 'L0_ffn_b1', 'L0_ffn_b2',
        'seg', 'L1_xattn_w_kv_comp', 'L1_xattn_w_q_down', 'quw', 'L1_xattn_w_k_up', 'L1_xattn_w_k_rope',
        'L1_xattn_w_v_up', 'wout', 'L1_ffn_w_fc', 'L1_ffn_w_proj', 'L1_ffn_gate', 'vt', 'u', 'fbt', 'trig', 'ktrig']


def rotary_table(n):
    half = R // 2
    inv = (1.0 / np.power(np.float32(10000.0), np.arange(half, dtype=np.float32) / np.float32(half))).astype(np.float32)
    ang = np.arange(n, dtype=np.float32)[:, None] * inv
    return np.stack([np.cos(ang), np.sin(ang)], axis=1).astype(np.float32)


def kernel(**inputs):
    import concourse.bacc as _bacc
    from concourse.bass_utils import run_bass_kernel_spmd as _run

    a = {k: np.asarray(v) for k, v in inputs.items()}
    for name in ('L0_xattn_Wq', 'L0_xattn_Wk', 'L0_xattn_Wv', 'L0_xattn_Wo'):
        a[name] = a[name].T
    for name in ('L0_xattn_bq', 'L0_xattn_bk'):
        a[name] = a[name].reshape(NG, P).T
    a['L0_ffn_b1'] = a['L0_ffn_b1'].reshape(B, NM, P).transpose(0, 2, 1)
    w1 = a['L0_ffn_w1'].reshape(B, NK, P, NM, P).transpose(0, 3, 2, 1, 4).reshape(B, NM, P, D)
    w2 = a['L0_ffn_w2'].reshape(B, NM, P, D)
    a['w12'] = np.concatenate([w1, w2], axis=3)
    a['seg'] = a['itok_BxS_0_511'].reshape(B, NT, P).transpose(0, 2, 1)
    up, rope = a['L1_xattn_w_q_up'], a['L1_xattn_w_q_rope']
    a['quw'] = np.concatenate([up[:, 0:512], rope[:, 0:512], up[:, 512:1024], rope[:, 512:1024]], axis=1)
    a['wout'] = a['L1_xattn_w_out'].reshape(2 * NK, P, D).transpose(1, 0, 2).reshape(P, 2 * NK * D)
    a['vt'] = a['L1_ffn_v'].T.reshape(NK, P, RANK).transpose(1, 0, 2).reshape(P, NK * RANK)
    a['u'] = a['L1_ffn_u'].reshape(NM, P, RANK).transpose(1, 0, 2)
    a['fbt'] = a['L1_ffn_fast_b'].T
    a['L1_ffn_gate'] = a['L1_ffn_gate'].reshape(1)
    a['trig'] = rotary_table(S).reshape(NT, P, 2, R // 2).transpose(1, 0, 2, 3)
    a['ktrig'] = rotary_table(KEYS)

    nc = _bacc.Bacc("TRN2", target_bir_lowering=False, num_devices=1)
    arrays, io = {}, {}
    for name in _INS:
        arrays[name] = np.ascontiguousarray(a[name])
        io[name] = nc.dram_tensor(name, arrays[name].shape, mybir.dt.from_np(arrays[name].dtype), kind="ExternalInput").ap()
    io["out"] = nc.dram_tensor("out", (B, S, D), F32, kind="ExternalOutput").ap()
    io["mid"] = nc.dram_tensor("mid", (B, S, D), F32, kind="Internal").ap()
    layer0(nc, io)
    layer1(nc, io)
    return _run(nc, [arrays], core_ids=[0]).results[0]["out"]
```

```python
from contextlib import ExitStack

import numpy as np

import concourse.bass as bass
from concourse import mybir

ALU = mybir.AluOpType
ACT = mybir.ActivationFunctionType
F32 = mybir.dt.float32
F16 = mybir.dt.float16
I32 = mybir.dt.int32
AX_X = mybir.AxisListType.X

P = 128
B = 8
S = 512
D = 512
NT = S // P
NK = D // P
KEYS = 120
EPS = 1e-5
WS = 64.0
LOWEST = -3.4028234663852886e38

H = 16
HD0 = D // H
HG = 4
NG = H // HG
STEPS = NT * NG
SLOTS = STEPS + 10
TOP = max(1, int(KEYS * 0.1))
EXP0 = float(1.0 / np.sqrt(np.float32(HD0))) / (WS * WS)
F = 2048
NM = F // P
PRO = 6
STATIONS = PRO + SLOTS
W2_LAG = 6
FREE = [k for k in range(PRO + 4, STATIONS) if k % 4 != 3]
MLP_AT = [[2 * k, 2 * k + 1] if k < PRO else [k + PRO] if k < PRO + 4 else
          [FREE.index(k) + NM] if k in FREE[:NM] else [] for k in range(STATIONS)]
HD = 64
R = 64
KVC = 128
QC = 192
QR = QC - P
LOOKBACK = 2
EXP1 = float(1.0 / np.sqrt(np.float32(HD + R))) / (WS * WS)
RANK = 16
ROUND = 12582912.0
GELU_C = float(np.sqrt(2.0 / np.pi))
GELU_A = 0.044715
ZROWS = 96


class Signal:

    def __init__(self, sem, per):
        self.sem = sem
        self.per = per

    def at(self, b, n):
        return b * self.per + (n + 1)


class Chain:

    def __init__(self, sem):
        self.sem, self.n = sem, 0

    def add(self, ins):
        self.n += 1
        ins.then_inc(self.sem, 1)
        return self.n


def prime(eng, signals):
    for s in signals:
        eng.sem_inc(s.sem, 1)


def wait(eng, s, b, n):
    eng.wait_ge(s.sem, s.at(b, n))


def layer0(nc, io):
    DVE_LINKS = 36
    with ExitStack() as ctx:
        sb = lambda name, shape, dt=F32: ctx.enter_context(nc.sbuf_tensor(name, shape, dt))
        pb = lambda name, dt=F32: ctx.enter_context(nc.psum_tensor(name, [P, 512], dt))
        sems = []

        def sem(name):
            sems.append(nc.alloc_semaphore(name))
            return sems[-1]

        sig = lambda name, per: Signal(sem(name), per)

        wq = [sb(f"wq{h}", [P, NK, D], F16) for h in "hl"]
        wk = [sb(f"wk{h}", [P, NK, D], F16) for h in "hl"]
        wv = [sb(f"wv{h}", [P, NK, D], F16) for h in "hl"]
        wo = [sb(f"wo{h}", [P, NK, D], F16) for h in "hl"]
        ident = sb("ident", [P, P])
        gates = sb("gates", [P, 4])
        gt = sb("gt", [P, 4])
        gs = sb("gs", [P, 4])
        bq = sb("bq", [P, NG])
        bk = sb("bk", [P, NG])
        bow = sb("bow", [P, D], F16)
        b2w = sb("b2w", [P, D], F16)
        upper = sb("upper", [P, P], F16)
        lower = sb("lower", [P, P], F16)
        half = sb("half", [P, 1])

        xin = sb("xin", [P, NT, D])
        xr = sb("xr", [P, NT, D])
        xb = sb("xb", [P, NT, D])
        xn = [sb(f"xn{i}", [P, D]) for i in range(2)]
        stat = sb("stat", [P, 8, 6])
        mean = sb("mean", [P, 8, 2])
        vare = sb("vare", [P, 8])
        rstd = sb("rstd", [P, 8])
        xta = [sb(f"xta{h}", [P, NK, S], F16) for h in "hl"]
        xtb = [sb(f"xtb{h}", [P, NK, S], F16) for h in "hl"]

        cx = sb("cx", [P, D])
        cxt = [sb(f"cxt{h}", [P, NK, KEYS], F16) for h in "hl"]
        kb = [sb(f"kb{h}", [P, NG, HG, KEYS], F16) for h in "hl"]
        v = sb("v", [P, D])
        qt = [sb(f"qt{h}", [P, NG, S], F16) for h in "hl"]
        sc = [sb(f"sc{i}", [P, HG, KEYS]) for i in range(2)]
        ex = [sb(f"ex{i}", [P, HG, KEYS]) for i in range(2)]
        pr = [sb(f"pr{i}", [P, HG, KEYS]) for i in range(2)]
        rep = sb("rep", [P, HG, KEYS])
        kf = rep
        top1 = [sb(f"top1{i}", [P, HG, 8]) for i in range(2)]
        top2 = [sb(f"top2{i}", [P, HG, 8]) for i in range(2)]
        rsum = sb("rsum", [P, NT, H])
        rinv = sb("rinv", [P, NT, H])
        pt = [sb(f"pt{i}", [P, HG, P]) for i in range(2)]
        ao = cx
        aot = [sb(f"aot{h}", [P, NK, P], F16) for h in "hl"]

        b1 = sb("b1", [P, NM])
        w1r = [sb(f"w1r{i}", [P, D]) for i in range(2)]
        w2r = [sb(f"w2r{i}", [P, D]) for i in range(2)]
        w1x = [[sb(f"w1x{i}{h}", [P, D], F16) for h in "hl"] for i in range(3)]
        w2x = [sb(f"w2x{h}", [P, NM, D], F16) for h in "hl"]
        hp = [sb(f"hp{i}", [P, S]) for i in range(2)]
        hu = [sb(f"hu{i}", [P, S]) for i in range(2)]
        b2 = hu[1]
        b1s = sb("b1s", [P, NM])
        hx = [sb(f"hx{h}", [P, NM, S], F16) for h in "hl"]
        wstage = [hx[i][:].bitcast(F32).rearrange("p m n -> p (m n)")[:, 0:NK * D] for i in range(2)]

        bT = [pb("bT0"), pb("bT1")]
        bS, bP, bO, bY = pb("bS"), pb("bP"), pb("bO"), pb("bY")
        bQ = [bS, bY]
        bM = [pb("bM0"), pb("bM1")]

        s_const = sem("s_const")
        s_w = [sem("s_w0"), sem("s_w1")]
        s_whi = sem("s_whi")
        s_wlo = sem("s_wlo")
        s_id0 = sem("s_id0")
        s_setup = sem("s_setup")
        s_tanh = sem("s_tanh")
        s_bias = sem("s_bias")
        ld_r = sem("ld_r")
        ld_x, ld_c, ld_b1, ld_b2 = sem("ld_x"), sem("ld_c"), sem("ld_b1"), sem("ld_b2")
        ld_w1 = [sem("ld_w10"), sem("ld_w11")]
        ld_w2 = [sem("ld_w20"), sem("ld_w21")]
        cxt_ps, k_ps, v_ps = sig("cxt_ps", 1), sig("k_ps", 1), sig("v_ps", 1)
        xt_ps, q_ps, s_ps, pt_ps = sig("xt_ps", 2 * NT), sig("q_ps", NG), sig("s_ps", STEPS), sig("pt_ps", STEPS)
        o_ps, ao_ps, y_ps = sig("o_ps", STEPS), sig("ao_ps", NT), sig("y_ps", NT)
        h_ps, z_ps = sig("h_ps", NM), sig("z_ps", NT)
        cx_hi, k_hi, q_hi, x_hi = sig("cx_hi", 1), sig("k_hi", 1), sig("q_hi", NG), sig("x_hi", 2 * NT)
        s_copy, e_done, pt_copy, ao_hi = sig("s_copy", STEPS), sig("e_done", STEPS), sig("pt_copy", STEPS), sig("ao_hi", NT)
        b2_hi = sig("b2_hi", 1)
        w1_hi, w2_hi, h_read, tanh_done = sig("w1_hi", NM), sig("w2_hi", NM), sig("h_read", NM), sig("tanh_done", NM)
        cx_lo, k_full, k_lo, v_done = sig("cx_lo", 1), sig("k_full", 1), sig("k_lo", 1), sig("v_done", 1)
        q_lo, x_lo, var_done, xn_done = sig("q_lo", NG), sig("x_lo", 2 * NT), sig("var_done", 2 * NT), sig("xn_done", 2 * NT)
        max_done, top_done, p_done, o_norm, ao_lo = sig("max_done", STEPS), sig("top_done", STEPS), sig("p_done", STEPS), sig("o_norm", NT), sig("ao_lo", NT)
        res1, res2 = sig("res1", NT), sig("res2", NT)
        w1_lo, w2_lo, h_hi, h_lo = sig("w1_lo", NM), sig("w2_lo", NM), sig("h_hi", NM), sig("h_lo", NM)
        b2_lo = sig("b2_lo", 1)
        gelu_done, b1s_done = sig("gelu_done", NM), sig("b1s_done", 1)
        dv = sig("dv", DVE_LINKS)
        shifted, rstd_done = sig("shifted", STEPS), sig("rstd_done", 2 * NT)
        cubed, arg_done = sig("cubed", NM), sig("arg_done", NM)
        x_out = sig("x_out", 16)

        block = ctx.enter_context(nc.Block())
        x_v = io["x"].rearrange("b (t p) d -> b p t d", p=P)
        mid_v = io["mid"].rearrange("b (t p) d -> b p t d", p=P)
        STAGED = [(io["L0_xattn_Wk"], wk), (io["L0_xattn_Wv"], wv), (io["L0_xattn_Wq"], wq), (io["L0_xattn_Wo"], wo)]
        four = lambda ap: ap.rearrange("p (k n) -> p k n", k=4)

        def turns(eng, turn):
            turn(0, None)
            with eng.Fori(0, B - 1) as c:
                turn(c + 1, c)
            turn(None, B - 1)

        @block.sync
        def _(sp):
            for n, (src, _) in enumerate(STAGED):
                if n >= 2:
                    sp.wait_ge(s_wlo, n - 1)
                sp.dma_start(four(wstage[n % 2]), src.rearrange("(k p) n -> p k n", p=P)).then_inc(s_w[n % 2], 16)

            def turn(b, c):
                def hold(s_, b, n):
                    wait(sp, s_, b, n)
                    sp.nop(nofuse=True)

                def load_w1(c, m):
                    hold(w1_lo, c, max(m - 1, 0))
                    sp.dma_start(w1r[m % 2][:], io["w1"][c, m]).then_inc(ld_w1[m % 2], 16)

                if c is not None:
                    hold(b1s_done, c, 0)
                    hold(h_read, c, 0)
                    sp.dma_start(b1[:], io["L0_ffn_b1"][c]).then_inc(ld_b1, 16)
                if b is not None:
                    hold(res1, b, 0)
                    sp.dma_start(cx[0:KEYS, :], io["ctx_1024"][b]).then_inc(ld_c, 16)
                    sp.dma_start(xin[:], x_v[b]).then_inc(ld_x, 16)
                if c is not None:
                    for m in range(2, NM + W2_LAG + 1):
                        if m < NM:
                            load_w1(c, m)
                        i = m - W2_LAG - 1
                        if i >= 0:
                            hold(w2_lo, c, max(i - 1, 0))
                            sp.dma_start(w2r[i % 2][:], io["w2"][c, i]).then_inc(ld_w2[i % 2], 16)
                        if m == 4:
                            hold(res1, c, NT)
                            sp.wait_ge(x_out.sem, c * 16 + 1)
                            sp.nop(nofuse=True)
                            sp.dma_start(xb[:], xr[:]).then_inc(ld_r, 16)
                        if m == NM + 2:
                            hold(h_lo, c, NM)
                            sp.dma_start(b2[0:1, :], io["L0_ffn_b2"][c].partition_broadcast(1)).then_inc(ld_b2, 16)

                if b is not None:
                    load_w1(b, 0)
                    load_w1(b, 1)

            turns(sp, turn)

        @block.gpsimd
        def _(pool):
            prime(pool, [shifted, rstd_done, cubed, arg_done])
            for dst, src in ((gates[:, 0:2], io["g_xattn"]), (gates[:, 2:4], io["g_ffn"]),):
                pool.dma_start(dst, src.partition_broadcast(P)).then_inc(s_const, 16)
            pool.dma_start(hp[0][0:1, :], io["L0_xattn_bo"].partition_broadcast(1)).then_inc(s_const, 16)
            pool.dma_start(hp[0][64:65, :], io["L0_xattn_bv"].partition_broadcast(1)).then_inc(s_const, 16)
            pool.dma_start(bq[:], io["L0_xattn_bq"]).then_inc(s_const, 16)
            pool.dma_start(bk[:], io["L0_xattn_bk"]).then_inc(s_const, 16)
            nc.gpsimd.memset(ident[:], 0.0).then_inc(s_id0, 1)
            nc.gpsimd.memset(kb[0][:], 0.0).then_inc(s_id0, 1)
            nc.gpsimd.memset(kb[1][:], 0.0).then_inc(s_id0, 1)
            nc.gpsimd.memset(half[:], -0.5).then_inc(s_id0, 1)
            nc.gpsimd.memset(upper[:], 0.0).then_inc(s_id0, 1)
            nc.gpsimd.memset(lower[:], 0.0).then_inc(s_id0, 1)
            nc.gpsimd.memset(bow[:], 0.0).then_inc(s_id0, 1)
            nc.gpsimd.memset(b2w[:], 0.0).then_inc(s_id0, 1)
            pool.wait_ge(s_id0, 8)
            nc.gpsimd.memset(upper[0:64, :], 1.0).then_inc(s_id0, 1)
            pool.wait_ge(s_id0, 9)
            nc.gpsimd.memset(lower[64:P, :], 1.0).then_inc(s_id0, 1)
            pool.wait_ge(s_id0, 10)
            nc.gpsimd.affine_select(out=ident[:], in_=ident[:], compare_op=ALU.not_equal, fill=1.0, base=0,
                                    pattern=[[-1, P]], channel_multiplier=1).then_inc(s_setup, 1)

            def turn(b, c):
                def power(n):
                    wait(pool, var_done, b, n + 1)
                    nc.gpsimd.tensor_tensor(rstd[:, n:n + 1], vare[:, n:n + 1], half[:], ALU.pow).then_inc(rstd_done.sem, 1)

                if b is not None:
                    for t in range(NT):
                        power(t)

                def attention(k):
                    s = k - PRO
                    if 0 <= s < STEPS:
                        wait(pool, max_done, b, s + 1)
                        if s >= 2:
                            wait(pool, p_done, b, s - 1)
                        nc.gpsimd.tensor_tensor(ex[s % 2][:], sc[s % 2][:],
                                                top1[s % 2][:, :, 0:1].to_broadcast([P, HG, KEYS]), ALU.subtract)\
                            .then_inc(shifted.sem, 1)
                    if s % 4 == 2 and 0 <= (s - 10) // 4 < NT:
                        power(NT + (s - 10) // 4)

                def mlp(k):
                    m = k - 1
                    if 0 <= m < NM:
                        wait(pool, h_read, c, m + 1)
                        nc.gpsimd.tensor_tensor(hu[m % 2][:], hu[m % 2][:], hp[m % 2][:], ALU.mult).then_inc(cubed.sem, 1)
                        wait(pool, cubed, c, m + 1)
                        nc.gpsimd.tensor_tensor(hu[m % 2][:], hu[m % 2][:], hp[m % 2][:], ALU.add).then_inc(arg_done.sem, 1)

                for k in range(STATIONS):
                    if b is not None:
                        attention(k)
                    if c is not None:
                        for n in MLP_AT[k]:
                            mlp(n)

            turns(pool, turn)

        @block.scalar
        def _(act):
            prime(act, [cx_hi, k_hi, q_hi, x_hi, s_copy, e_done, pt_copy, ao_hi, w1_hi, w2_hi, h_read, tanh_done, b2_hi])
            act.sem_inc(x_out.sem, 1)
            act.wait_ge(s_const, 96)
            nc.scalar.activation(gt[:], gates[:], ACT.Tanh).then_inc(s_tanh, 1)
            act.wait_ge(s_setup, 1)
            for q in (0, 64):
                nc.scalar.activation(bow[q:q + 1, :], hp[0][q:q + 1, :], ACT.Copy, scale=WS).then_inc(s_tanh, 1)
            for n, (_, w) in enumerate(STAGED):
                act.wait_ge(s_w[n % 2], 16 * (n // 2 + 1))
                nc.scalar.activation(w[0][:].rearrange("p k n -> p (k n)"), wstage[n % 2], ACT.Copy, scale=WS).then_inc(s_whi, 1)

            def turn(b, c):
                def x_high(n):
                    wait(act, xt_ps, b, n + 1)
                    t, u = n % NT, (1 + n if n < NT else 1)
                    xt = xta if n < NT else xtb
                    if n == NT and c is not None:
                        wait(act, h_ps, c, NM)
                    nc.scalar.activation(xt[0][:, :, t * P:(t + 1) * P], four(bT[u % 2][:]), ACT.Copy).then_inc(x_hi.sem, 1)

                def q_high(g):
                    wait(act, q_ps, b, g + 1)
                    nc.scalar.activation(qt[0][:, g, :], bQ[g % 2][:], ACT.Identity, bias=bq[:, g:g + 1]).then_inc(q_hi.sem, 1)

                def w1_high(c, m):
                    act.wait_ge(ld_w1[m % 2], c * (16 * NM // 2) + 16 * (m // 2 + 1))
                    if m >= 3:
                        wait(act, h_ps, c, m - 2)
                    nc.scalar.activation(w1x[m % 3][0][:], w1r[m % 2][:], ACT.Copy, scale=WS).then_inc(w1_hi.sem, 1)

                def attention(k):
                    s = k - PRO
                    if k == 0:
                        wait(act, cxt_ps, b, 1)
                        nc.scalar.activation(cxt[0][:], four(bT[0][:, 0:NK * KEYS]), ACT.Copy).then_inc(cx_hi.sem, 1)
                    if k == 1:
                        wait(act, k_full, b, 1)
                        for j in range(HG):
                            r = slice(j * HD0, (j + 1) * HD0)
                            ins = nc.scalar.activation(kb[0][r, :, j, :], kf[r, :, :], ACT.Copy)
                        ins.then_inc(k_hi.sem, 1)
                    if k in (2, 3):
                        x_high(2 * k - 4)
                        x_high(2 * k - 3)
                    if k in (4, 5):
                        q_high(2 * k - 8)
                        q_high(2 * k - 7)
                    if 0 <= s < STEPS:
                        wait(act, s_ps, b, s + 1)
                        if s >= 2:
                            wait(act, p_done, b, s - 1)
                        nc.scalar.activation(sc[s % 2][:], four(bS[:, 0:HG * KEYS]), ACT.Copy).then_inc(s_copy.sem, 1)
                    if 1 <= s <= STEPS:
                        wait(act, shifted, b, s)
                        e = ex[(s - 1) % 2]
                        nc.scalar.activation(e[:], e[:], ACT.Exp, scale=EXP0).then_inc(e_done.sem, 1)
                    if 2 <= s < STEPS + 2:
                        i = s - 2
                        wait(act, pt_ps, b, i + 1)
                        if i >= 2:
                            wait(act, o_ps, b, i - 1)
                        nc.scalar.activation(pt[i % 2][0:KEYS], four(bP[0:KEYS, :]), ACT.Copy).then_inc(pt_copy.sem, 1)
                    if s % 4 == 0 and 0 <= (s - 8) // 4 < NT:
                        t = (s - 8) // 4
                        wait(act, ao_ps, b, t + 1)
                        if t:
                            wait(act, y_ps, b, t)
                        nc.scalar.activation(aot[0][:], four(bT[0][:]), ACT.Copy).then_inc(ao_hi.sem, 1)
                    if s % 4 == 1 and 0 <= (s - 13) // 4 < NT:
                        x_high(NT + (s - 13) // 4)
                    if k == STATIONS - 2:
                        wait(act, h_ps, b, 0)
                        w1_high(b, 0)

                def mlp(k):
                    if k + 1 < NM:
                        w1_high(c, k + 1)
                    if 2 <= k < NM + 2:
                        m = k - 2
                        wait(act, arg_done, c, m + 1)
                        nc.scalar.activation(hu[m % 2][:], hu[m % 2][:], ACT.Tanh, scale=GELU_C).then_inc(tanh_done.sem, 1)
                    if 1 <= k < NM + 1:
                        m = k - 1
                        wait(act, h_ps, c, m + 1)
                        if m == 0:
                            wait(act, b1s_done, c, 1)
                        if m >= 2:
                            wait(act, h_lo, c, m - 1)
                        if m == 1:
                            wait(act, b2_lo, c, 0)
                        nc.scalar.activation(hp[m % 2][:], bM[m % 2][:], ACT.Identity, bias=b1[:, m:m + 1], scale=1 / WS)
                        nc.scalar.activation(hu[m % 2][:], bM[m % 2][:], ACT.Square, bias=b1s[:, m:m + 1],
                                             scale=float(np.sqrt(GELU_A)) / WS).then_inc(h_read.sem, 1)
                    if k == NM + 5:
                        act.wait_ge(ld_b2, c * 16 + 16)
                        nc.scalar.activation(b2w[0:1, :], b2[0:1, :], ACT.Copy, scale=2 * WS).then_inc(b2_hi.sem, 1)
                    if W2_LAG <= k < NM + W2_LAG:
                        i = k - W2_LAG
                        if i == 0:
                            wait(act, z_ps, c, 0)
                        act.wait_ge(ld_w2[i % 2], c * (16 * NM // 2) + 16 * (i // 2 + 1))
                        nc.scalar.activation(w2x[0][:, i, :], w2r[i % 2][:], ACT.Copy, scale=WS).then_inc(w2_hi.sem, 1)

                for k in range(STATIONS):
                    if b is not None:
                        attention(k)
                    if c is not None:
                        for n in MLP_AT[k]:
                            mlp(n)
                if c is not None:
                    wait(act, res2, c, NT)
                    act.dma_start(mid_v[c], xb[:]).then_inc(x_out.sem, 16)

            turns(act, turn)
            act.wait_ge(x_out.sem, B * 16 + 1)

        @block.tensor
        def _(pe):
            prime(pe, [cxt_ps, k_ps, v_ps, xt_ps, q_ps, s_ps, pt_ps, o_ps, ao_ps, y_ps, h_ps, z_ps])
            mm = nc.tensor.matmul

            def product(out, lhs, rhs, k, n):
                mm(out, lhs(0), rhs(0), start=(k == 0), stop=False)
                mm(out, lhs(0), rhs(1), start=False, stop=False)
                return mm(out, lhs(1), rhs(0), start=False, stop=(k == n - 1))

            pe.wait_ge(s_setup, 1)
            pe.wait_ge(s_bias, 4)
            pe.wait_ge(s_wlo, len(STAGED))

            def turn(b, c):
                def x_transpose(n):
                    u = 1 + n if n < NT else 1
                    wait(pe, xn_done, b, n + 1)
                    if u == 2:
                        wait(pe, cx_lo, b, 1)
                    elif n >= 2:
                        wait(pe, x_lo, b, n - 1 if n < NT else n)
                    for k in range(NK):
                        ins = nc.tensor.transpose(bT[u % 2][:, k * P:(k + 1) * P], xn[n % 2][:, k * P:(k + 1) * P], ident[:])
                    ins.then_inc(xt_ps.sem, 1)

                def queries(g):
                    if g == 0:
                        wait(pe, x_lo, b, NT)
                        wait(pe, k_full, b, 1)
                    elif g == 1:
                        wait(pe, v_done, b, 1)
                    else:
                        wait(pe, q_lo, b, g - 1)
                    for k in range(NK):
                        ins = product(bQ[g % 2][:], lambda h: wq[h][:, k, g * P:(g + 1) * P], lambda h: xta[h][:, k, :], k, NK)
                    ins.then_inc(q_ps.sem, 1)

                def attention(k_):
                    s = k_ - PRO
                    if k_ == 0:
                        pe.wait_ge(ld_c, b * 16 + 16)
                        for k in range(NK):
                            ins = nc.tensor.transpose(bT[0][:, k * KEYS:(k + 1) * KEYS], cx[0:KEYS, k * P:(k + 1) * P],
                                                      ident[0:KEYS, 0:KEYS])
                        ins.then_inc(cxt_ps.sem, 1)
                    if k_ == 1:
                        wait(pe, cx_lo, b, 1)
                        for g in range(NG):
                            for k in range(NK):
                                ins = product(bS[:, g * KEYS:(g + 1) * KEYS], lambda h: wk[h][:, k, g * P:(g + 1) * P],
                                              lambda h: cxt[h][:, k, :], k, NK)
                        ins.then_inc(k_ps.sem, 1)
                        for k in range(NK):
                            product(bY[0:KEYS, :], lambda h: cxt[h][:, k, :], lambda h: wv[h][:, k, :], k, NK + 1)
                        mm(bY[0:KEYS, :], lower[:, 0:KEYS], bow[:], start=False, stop=True).then_inc(v_ps.sem, 1)
                    if k_ in (2, 3):
                        x_transpose(2 * k_ - 4)
                        x_transpose(2 * k_ - 3)
                    if k_ in (4, 5):
                        queries(2 * k_ - 8)
                        queries(2 * k_ - 7)
                    if 0 <= s < STEPS:
                        t, g = s // NG, s % NG
                        if s == 0:
                            wait(pe, k_lo, b, 1)
                            wait(pe, q_lo, b, NG)
                        else:
                            wait(pe, s_copy, b, s)
                        product(bS[:, 0:HG * KEYS], lambda h: qt[h][:, g, t * P:(t + 1) * P],
                                lambda h: kb[h][:, g].rearrange("p h n -> p (h n)"), 0, 1).then_inc(s_ps.sem, 1)
                    if 2 <= s < STEPS + 2:
                        i = s - 2
                        wait(pe, p_done, b, i + 1)
                        if i:
                            wait(pe, pt_copy, b, i)
                        for j in range(HG):
                            ins = nc.tensor.transpose(bP[0:KEYS, j * P:(j + 1) * P], pr[i % 2][:, j, :], ident[:])
                        ins.then_inc(pt_ps.sem, 1)
                    if 3 <= s < STEPS + 3:
                        i = s - 3
                        t, g = i // NG, i % NG
                        wait(pe, pt_copy, b, i + 1)
                        if g == 0 and t:
                            wait(pe, o_norm, b, t)
                        for j in range(HG):
                            col = (g * HG + j) * HD0
                            ins = mm(bO[:, col:col + HD0], pt[i % 2][0:KEYS, j, :], v[0:KEYS, col:col + HD0],
                                     start=True, stop=True)
                        ins.then_inc(o_ps.sem, 1)
                    if s % 4 == 0 and 0 <= (s - 8) // 4 < NT:
                        t = (s - 8) // 4
                        wait(pe, o_norm, b, t + 1)
                        if t == 0:
                            wait(pe, x_lo, b, NT)
                        else:
                            wait(pe, ao_lo, b, t)
                        for k in range(NK):
                            ins = nc.tensor.transpose(bT[0][:, k * P:(k + 1) * P], ao[:, k * P:(k + 1) * P], ident[:])
                        ins.then_inc(ao_ps.sem, 1)
                    if s % 4 == 1 and 0 <= (s - 9) // 4 < NT:
                        t = (s - 9) // 4
                        wait(pe, ao_lo, b, t + 1)
                        if t:
                            wait(pe, res1, b, t)
                        for k in range(NK):
                            product(bY[:], lambda h: aot[h][:, k, :], lambda h: wo[h][:, k, :], k, NK + 1)
                        mm(bY[:], upper[:], bow[:], start=False, stop=True).then_inc(y_ps.sem, 1)
                    if s % 4 == 0 and 0 <= (s - 12) // 4 < NT:
                        x_transpose(NT + (s - 12) // 4)

                def mlp(m):
                    if m < NM:
                        wait(pe, w1_lo, c, m + 1)
                        if m == 0:
                            wait(pe, x_lo, c, 2 * NT)
                            wait(pe, res2, c, 0)
                        if m >= 2:
                            wait(pe, h_read, c, m - 1)
                        for k in range(NK):
                            ins = product(bM[m % 2][:], lambda h: w1x[m % 3][h][:, k * P:(k + 1) * P],
                                          lambda h: xtb[h][:, k, :], k, NK)
                        ins.then_inc(h_ps.sem, 1)
                    else:
                        j = m - NM
                        t, part = 2 * (j // 8) + j % 2, j % 8 // 2
                        if j < 8 and j % 2 == 0:
                            wait(pe, h_lo, c, 4 * part + 4)
                            wait(pe, w2_lo, c, 4 * part + 4)
                        if j < 2:
                            wait(pe, h_read, c, NM)
                        elif part == 0:
                            wait(pe, res2, c, t - 1)
                        for i in range(4 * part, 4 * part + 4):
                            product(bM[t % 2][:], lambda h: hx[h][:, i, t * P:(t + 1) * P], lambda h: w2x[h][:, i, :], i, NM + 1)
                        if part == 3:
                            wait(pe, b2_lo, c, 1)
                            mm(bM[t % 2][:], upper[:], b2w[:], start=False, stop=True).then_inc(z_ps.sem, 1)

                for k in range(STATIONS):
                    if b is not None:
                        attention(k)
                    if c is not None:
                        for n in MLP_AT[k]:
                            mlp(n)

            turns(pe, turn)

        @block.vector
        def _(dve):
            vec = nc.vector
            chain = Chain(dv.sem)
            prime(dve, [cx_lo, k_full, k_lo, v_done, q_lo, x_lo, var_done, xn_done, top_done, p_done, o_norm, ao_lo,
                        res1, res2, w1_lo, w2_lo, h_hi, h_lo, gelu_done, b1s_done, max_done, b2_lo, dv])
            dve.wait_ge(s_const, 96)
            vec.tensor_scalar(bq[:], bq[:], WS, None, ALU.mult).then_inc(s_bias, 1)
            vec.tensor_scalar(bk[:], bk[:], WS, None, ALU.mult).then_inc(s_bias, 1)
            dve.wait_ge(s_tanh, 1)
            vec.tensor_scalar(gs[:, 0:2], gt[:, 0:2], 1 / WS, None, ALU.mult)
            vec.tensor_scalar(gs[:, 2:4], gt[:, 2:4], 0.5 / WS, None, ALU.mult).then_inc(s_bias, 1)
            dve.wait_ge(s_tanh, 3)
            dve.wait_ge(s_setup, 1)
            for q in (0, 64):
                ins = vec.scalar_tensor_tensor(bow[q + 32:q + 33, :], hp[0][q:q + 1, :], WS, bow[q:q + 1, :], ALU.mult,
                                               ALU.subtract)
            ins.then_inc(s_bias, 1)
            for n, (_, w) in enumerate(STAGED):
                dve.wait_ge(s_whi, n + 1)
                vec.scalar_tensor_tensor(w[1][:].rearrange("p k n -> p (k n)"), wstage[n % 2], WS,
                                         w[0][:].rearrange("p k n -> p (k n)"), ALU.mult, ALU.subtract).then_inc(s_wlo, 1)
            dve.wait_ge(s_bias, 4)
            dve.wait_ge(s_setup, 1)

            def turn(b, c):
                chain.n = 0

                def after(n):
                    wait(dve, dv, b, n)

                def hold(s_, n):
                    wait(dve, s_, b, n)
                    dve.nop(nofuse=True)

                def stats(n, src):
                    i = chain.add(vec.bn_stats(stat[:, n, :], src))
                    hold(dv, i)
                    i = chain.add(vec.bn_aggr(mean[:, n, :], stat[:, n, :]))
                    after(i)
                    vec.tensor_scalar(vare[:, n:n + 1], mean[:, n, 1:2], EPS, None, ALU.add).then_inc(var_done.sem, 1)

                def normalise(n, src):
                    wait(dve, rstd_done, b, n + 1)
                    if n >= 2:
                        wait(dve, xt_ps, b, n - 1)
                    vec.tensor_scalar(xn[n % 2][:], src, mean[:, n, 0:1], rstd[:, n:n + 1], ALU.subtract, ALU.mult)\
                        .then_inc(xn_done.sem, 1)

                def x_low(n):
                    t, u = n % NT, (1 + n if n < NT else 1)
                    xt = xta if n < NT else xtb
                    wait(dve, x_hi, b, n + 1)
                    vec.tensor_tensor(xt[1][:, :, t * P:(t + 1) * P], four(bT[u % 2][:]), xt[0][:, :, t * P:(t + 1) * P],
                                      ALU.subtract).then_inc(x_lo.sem, 1)

                def q_low(g):
                    wait(dve, q_hi, b, g + 1)
                    vec.scalar_tensor_tensor(qt[1][:, g, :], bQ[g % 2][:], bq[:, g:g + 1], qt[0][:, g, :], ALU.add,
                                             ALU.subtract).then_inc(q_lo.sem, 1)

                def w1_low(c, m):
                    wait(dve, w1_hi, c, m + 1)
                    vec.scalar_tensor_tensor(w1x[m % 3][1][:], w1r[m % 2][:], WS, w1x[m % 3][0][:], ALU.mult, ALU.subtract)\
                        .then_inc(w1_lo.sem, 1)

                def attention(k):
                    s = k - PRO
                    if k == 0:
                        wait(dve, cx_hi, b, 1)
                        vec.tensor_tensor(cxt[1][:], four(bT[0][:, 0:NK * KEYS]), cxt[0][:], ALU.subtract).then_inc(cx_lo.sem, 1)
                        dve.wait_ge(ld_x, b * 16 + 16)
                        for t in range(NT):
                            stats(t, xin[:, t, :])
                        for t in range(2):
                            normalise(t, xin[:, t, :])
                    if k == 1:
                        wait(dve, k_ps, b, 1)
                        vec.tensor_tensor(kf[:], four(bS[:, 0:NG * KEYS]), bk[:].unsqueeze(2).to_broadcast([P, NG, KEYS]), ALU.add)\
                            .then_inc(k_full.sem, 1)
                        wait(dve, v_ps, b, 1)
                        vec.tensor_scalar(v[0:KEYS, :], bY[0:KEYS, :], 1 / WS, None, ALU.mult).then_inc(v_done.sem, 1)
                        wait(dve, k_hi, b, 1)
                        for j in range(HG):
                            r = slice(j * HD0, (j + 1) * HD0)
                            ins = vec.tensor_tensor(kb[1][r, :, j, :], kf[r, :, :], kb[0][r, :, j, :], ALU.subtract)
                        ins.then_inc(k_lo.sem, 1)
                    if k in (2, 3):
                        for t in (2 * k - 4, 2 * k - 3):
                            x_low(t)
                            if t < 2:
                                normalise(t + 2, xin[:, t + 2, :])
                    if k in (4, 5):
                        q_low(2 * k - 8)
                        q_low(2 * k - 7)
                    if s % 4 == 3 and 0 <= (s - 7) // 4 < NT:
                        t = (s - 7) // 4
                        wait(dve, p_done, b, NG * (t + 1))
                        i = chain.add(vec.reciprocal(rinv[:, t, :], rsum[:, t, :]))
                        after(i)
                        wait(dve, o_ps, b, NG * (t + 1))
                        if t:
                            wait(dve, ao_ps, b, t)
                        else:
                            wait(dve, cxt_ps, b, 1)
                        vec.tensor_tensor(ao[:].rearrange("p (h d) -> p h d", h=H), bO[:].rearrange("p (h d) -> p h d", h=H),
                                          rinv[:, t, :].unsqueeze(2).to_broadcast([P, H, HD0]), ALU.mult)\
                            .then_inc(o_norm.sem, 1)
                    if 0 <= s < STEPS:
                        if s == 0:
                            wait(dve, k_lo, b, 1)
                        hold(s_copy, s + 1)
                        if s >= 2:
                            hold(p_done, s - 1)
                        for j in range(HG):
                            ins = vec.max(top1[s % 2][:, j, :], sc[s % 2][:, j, :])
                        ins.then_inc(max_done.sem, 1)
                        hold(max_done, s + 1)
                        for j in range(HG):
                            ins = vec.match_replace(rep[:, j, :], top1[s % 2][:, j, :], sc[s % 2][:, j, :], LOWEST)
                        hold(dv, chain.add(ins))
                        for j in range(HG):
                            ins = vec.max(top2[s % 2][:, j, :], rep[:, j, :])
                        ins.then_inc(top_done.sem, 1)
                    if 1 <= s <= STEPS:
                        i = s - 1
                        t, g = i // NG, i % NG
                        wait(dve, e_done, b, i + 1)
                        wait(dve, top_done, b, i + 1)
                        if i >= 2:
                            wait(dve, pt_ps, b, i - 1)
                        for j in range(HG):
                            h = g * HG + j
                            ins = vec.scalar_tensor_tensor(pr[i % 2][:, j, :], sc[i % 2][:, j, :],
                                                           top2[i % 2][:, j, TOP - 9:TOP - 8], ex[i % 2][:, j, :],
                                                           ALU.is_ge, ALU.mult, accum_out=rsum[:, t, h:h + 1])
                        ins.then_inc(p_done.sem, 1)
                    if s % 4 == 0 and 0 <= (s - 8) // 4 < NT:
                        t = (s - 8) // 4
                        wait(dve, ao_hi, b, t + 1)
                        vec.tensor_tensor(aot[1][:], four(bT[0][:]), aot[0][:], ALU.subtract).then_inc(ao_lo.sem, 1)
                    if s % 4 == 2 and 0 <= (s - 10) // 4 < NT:
                        t = (s - 10) // 4
                        wait(dve, y_ps, b, t + 1)
                        if t == 0 and c is not None:
                            dve.wait_ge(ld_r, c * 16 + 16)
                        vec.scalar_tensor_tensor(xr[:, t, :], bY[:], gs[:, 0:1], xin[:, t, :], ALU.mult, ALU.add)\
                            .then_inc(res1.sem, 1)
                        wait(dve, res1, b, t + 1)
                        stats(NT + t, xr[:, t, :])
                    if s % 4 == 3 and 0 <= (s - 11) // 4 < NT:
                        t = (s - 11) // 4
                        normalise(NT + t, xr[:, t, :])
                    if s % 4 == 1 and 0 <= (s - 13) // 4 < NT:
                        x_low(NT + (s - 13) // 4)
                    if k == STATIONS - 2:
                        w1_low(b, 0)

                def hidden(m):
                    x = hp[m % 2]
                    wait(dve, tanh_done, c, m + 1)
                    vec.scalar_tensor_tensor(x[:], hu[m % 2][:], 1.0, x[:], ALU.add, ALU.mult).then_inc(gelu_done.sem, 1)
                    wait(dve, gelu_done, c, m + 1)
                    vec.tensor_copy(hx[0][:, m, :], x[:]).then_inc(h_hi.sem, 1)
                    wait(dve, h_hi, c, m + 1)
                    vec.tensor_tensor(hx[1][:, m, :], x[:], hx[0][:, m, :], ALU.subtract).then_inc(h_lo.sem, 1)

                def output(t):
                    wait(dve, z_ps, c, t + 1)
                    dve.wait_ge(ld_r, c * 16 + 16)
                    vec.scalar_tensor_tensor(xb[:, t, :], bM[t % 2][:], gs[:, 2:3], xb[:, t, :], ALU.mult, ALU.add)\
                        .then_inc(res2.sem, 1)

                def mlp(k):
                    if k + 1 < NM:
                        w1_low(c, k + 1)
                    if 2 <= k < NM + 2:
                        hidden(k - 2)
                    if k == NM + 5:
                        wait(dve, b2_hi, c, 1)
                        vec.scalar_tensor_tensor(b2w[32:33, :], b2[0:1, :], 2 * WS, b2w[0:1, :], ALU.mult, ALU.subtract)\
                            .then_inc(b2_lo.sem, 1)
                    if W2_LAG <= k < NM + W2_LAG:
                        i = k - W2_LAG
                        wait(dve, w2_hi, c, i + 1)
                        vec.scalar_tensor_tensor(w2x[1][:, i, :], w2r[i % 2][:], WS, w2x[0][:, i, :], ALU.mult, ALU.subtract)\
                            .then_inc(w2_lo.sem, 1)
                    if k in (NM + 7, NM + 8, NM + 15):
                        output({NM + 7: 0, NM + 8: 1, NM + 15: 2}[k])

                if c is not None:
                    dve.wait_ge(ld_b1, c * 16 + 16)
                    wait(dve, h_read, c, 0)
                    vec.tensor_scalar(b1s[:], b1[:], float(np.sqrt(GELU_A)), None, ALU.mult).then_inc(b1s_done.sem, 1)
                for k in range(STATIONS):
                    if c is not None and k == 0:
                        for n in MLP_AT[k]:
                            mlp(n)
                    if b is not None:
                        attention(k)
                    if c is not None and k:
                        for n in MLP_AT[k]:
                            mlp(n)
                if c is not None:
                    output(NT - 1)
                assert b is None or chain.n == DVE_LINKS, chain.n

            turns(dve, turn)

    nc.clear_and_free_semaphores(sems)
    nc.all_engine_barrier()


def layer1(nc, io):
    DVE_LINKS = 32
    with ExitStack() as ctx:
        sb = lambda name, shape, dt=F32: ctx.enter_context(nc.sbuf_tensor("l1_" + name, shape, dt))
        pb = lambda name, dt=F32: ctx.enter_context(nc.psum_tensor("l1_" + name, [P, 512], dt))
        sem = lambda name: ctx.enter_context(nc.semaphore("l1_" + name))
        sig = lambda name, per: Signal(sem(name), per)
        pair = lambda name, shape: [sb(name + h, shape, F16) for h in "hl"]

        kvw = pair("kvw", [P, NK, KVC])
        qdw = pair("qdw", [P, NK, QC])
        quw = pair("quw", [P, 2, 4, 512])
        kuw = pair("kuw", [P, H * HD])
        krw = pair("krw", [P, R])
        vuw = pair("vuw", [P, H * HD])
        ow = pair("ow", [P, 2 * NK, D])
        fcw = sb("fcw", [P, NK, F], F16)
        prw = sb("prw", [P, NM, D], F16)
        lru = sb("lru", [P, F], F16)
        lrz = sb("lrz", [P, S], F16)
        vw = pair("vw", [P, NK, RANK])
        fbw = sb("fbw", [RANK, RANK])
        fsc = sb("fsc", [P, NM])
        gsc = sb("gsc", [P, D])
        gs = sb("gs", [P, 4])
        ident = sb("ident", [P, P])
        half = sb("half", [P, 1])
        keyno = sb("keyno", [P, KEYS])
        trig = sb("trig", [P, NT, 2, R // 2])
        ktrig = sb("ktrig", [P, 2, R // 2])

        xin = sb("xin", [P, NT, D])
        xr = sb("xr", [P, NT, D])
        xo = sb("xo", [P, NT, D])
        xn = [sb(f"xn{i}", [P, D]) for i in range(2)]
        stat = sb("stat", [P, 8, 6])
        mean = sb("mean", [P, 8, 2])
        vare = sb("vare", [P, 8])
        rstd = sb("rstd", [P, 8])
        xta = pair("xta", [P, NK, S])
        xtb = pair("xtb", [P, NK, S])
        cx = sb("cx", [P, D])
        cxt = pair("cxt", [P, NK, KEYS])
        kvt = pair("kvt", [P, KEYS])
        krm = sb("krm", [P, 2, 2, R // 2])
        kr = sb("kr", [P, R])
        kc = pair("kc", [P, H, KEYS])
        vc = sb("vc", [P, H * HD])
        qct = pair("qct", [P, 2, S])
        qk = sb("qk", [P, H, P])
        rm = [sb(f"rm{i}", [P, 8, 2, R // 2]) for i in range(2)]
        qkt = pair("qkt", [P, H, P])
        segi = sb("segi", [P, NT], I32)
        segf = sb("segf", [P, NT])
        okay = sb("okay", [P, NT, KEYS])
        pen = sb("pen", [P, NT, KEYS])
        sc = [sb(f"sc{i}", [P, HG, KEYS]) for i in range(2)]
        ex = [sb(f"ex{i}", [P, HG, KEYS]) for i in range(3)]
        smax = sb("smax", [P, 2, HG])
        rsum = sb("rsum", [P, NT, H])
        rinv = sb("rinv", [P, NT, H])
        pt = [sb(f"pt{i}", [P, HG, P]) for i in range(2)]
        ao = sb("ao", [P, 2 * D])
        aot = pair("aot", [P, 2 * NK, P])
        rl = [sb(f"rl{i}", [P, S]) for i in range(2)]
        hx = [pair(f"hx{i}", [P, S]) for i in range(2)]
        zf = sb("zf", [RANK, S])

        bT = [pb("bT0"), pb("bT1")]
        bS, bW = pb("bS"), pb("bW")
        bP, bU, bO, bY = pb("bP"), pb("bU"), pb("bO"), pb("bY")
        bM = [bS, bW]
        acc = [bU, bP, bO, bY]
        x_v = io["mid"].rearrange("b (t p) d -> b p t d", p=P)
        out_v = io["out"].rearrange("b (t p) d -> b p t d", p=P)

        with ExitStack() as sctx:
            ssem = lambda name: sctx.enter_context(nc.semaphore("l1s_" + name))
            stage = [x[:].rearrange("p t n -> p (t n)") for x in (xo, xr, xin)]
            NB = len(stage)
            rounded = qk[:].rearrange("p h n -> p (h n)")
            tern = ao[:].bitcast(F16)
            small = xn[1]
            gates, gt, gate = small[:, 0:4], small[:, 4:8], small[:, 8:9]
            asum, scale, inv = small[:, 16:36], small[:, 48:68], small[:, 80:100]
            vraw = small[:, 128:128 + NK * RANK]
            diag = rl[0][:, 0:P]
            ones = rl[0][:, P:2 * P]
            u = hx[0][0][:].bitcast(F32).rearrange("p (m r) -> p m r", m=NM)
            us = hx[0][1][:].bitcast(F32).rearrange("p (m r) -> p m r", m=NM)
            ident16 = rl[1][:].bitcast(F16)[:, 0:P]

            flat = lambda w, h: w[h][:]
            SPLIT = [
                (io["L1_xattn_w_kv_comp"], P, NK * KVC, [flat(kvw, h).rearrange("p k n -> p (k n)") for h in (0, 1)]),
                (io["L1_xattn_w_q_down"], P, NK * QC, [flat(qdw, h).rearrange("p k n -> p (k n)") for h in (0, 1)]),
                (io["quw"][0:P], P, 2048, [flat(quw, h)[:, 0].rearrange("p u n -> p (u n)") for h in (0, 1)]),
                (io["quw"][P:2 * P], P, 2048, [flat(quw, h)[:, 1].rearrange("p u n -> p (u n)") for h in (0, 1)]),
                (io["L1_xattn_w_k_up"], P, H * HD, [flat(kuw, h) for h in (0, 1)]),
                (io["L1_xattn_w_k_rope"], P, R, [flat(krw, h) for h in (0, 1)]),
                (io["L1_xattn_w_v_up"], P, H * HD, [flat(vuw, h) for h in (0, 1)]),
                (io["wout"][:, 0:2048], P, 2048, [flat(ow, h)[:, 0:NK].rearrange("p k n -> p (k n)") for h in (0, 1)]),
                (io["wout"][:, 2048:4096], P, 2048, [flat(ow, h)[:, NK:2 * NK].rearrange("p k n -> p (k n)") for h in (0, 1)]),
            ]
            NS = len(SPLIT)
            NTERN = 8
            s_const, s_c2 = ssem("const"), ssem("c2")
            s_ld = [ssem(f"ld{i}") for i in range(NB)]
            s_hi, s_lo = ssem("hi"), ssem("lo")
            s_abs, s_scale, s_round, s_clip = ssem("abs"), ssem("scale"), ssem("round"), ssem("clip")
            s_tern, s_tps, s_tev = ssem("tern"), ssem("tps"), ssem("tev")
            s_id, s_tanh, s_small, s_us = ssem("id"), ssem("tanh"), ssem("small"), ssem("us")
            s_ups, s_uhi, s_ulo = ssem("ups"), ssem("uhi"), ssem("ulo")
            s_diag, s_gps, s_g = ssem("diag"), ssem("gps"), ssem("g")
            block = sctx.enter_context(nc.Block())

            @block.sync
            def _(sp):
                for n in range(NS + NTERN):
                    if n >= NB:
                        last = n - NB
                        if last < NS:
                            sp.wait_ge(s_lo, last + 1)
                        else:
                            sp.wait_ge(s_round, last + 1 - NS)
                    if n < NS:
                        src, rows, cols, _ = SPLIT[n]
                        if n < 2:
                            dst = stage[n][:, 0:cols].rearrange("p (k n) -> p k n", k=NK)
                            src = src.rearrange("(k p) n -> p k n", p=P)
                        else:
                            dst = stage[n % NB][0:rows, 0:cols]
                        sp.dma_start(dst, src).then_inc(s_ld[n % NB], 16)
                    else:
                        c = n - NS
                        if c < 4:
                            src = io["L1_ffn_w_fc"][c * 4 * P:(c + 1) * 4 * P, :].rearrange("(m p) n -> p m n", p=P)
                            sp.dma_start(stage[n % NB].rearrange("p (m n) -> p m n", m=4), src).then_inc(s_ld[n % NB], 16)
                        else:
                            c -= 4
                            sp.dma_start(stage[n % NB], io["L1_ffn_w_proj"][c * P:(c + 1) * P, :]).then_inc(s_ld[n % NB], 16)

            @block.gpsimd
            def _(pool):
                for dst, src in ((gates[:, 0:2], io["g_xattn"]), (gates[:, 2:4], io["g_ffn"]), (gate, io["L1_ffn_gate"])):
                    pool.dma_start(dst, src.partition_broadcast(P)).then_inc(s_const, 16)
                pool.dma_start(trig[:], io["trig"]).then_inc(s_const, 16)
                pool.dma_start(ktrig[0:KEYS], io["ktrig"]).then_inc(s_const, 16)
                pool.dma_start(vraw, io["vt"]).then_inc(s_const, 16)
                pool.dma_start(u, io["u"]).then_inc(s_const, 16)
                pool.dma_start(fbw[:], io["fbt"]).then_inc(s_const, 16)
                nc.gpsimd.memset(ident[:], 0.0).then_inc(s_c2, 1)
                nc.gpsimd.memset(half[:], -0.5).then_inc(s_id, 1)
                nc.gpsimd.memset(ones, 1.0).then_inc(s_id, 1)
                nc.gpsimd.memset(lru[:], 0.0).then_inc(s_id, 1)
                nc.gpsimd.memset(lrz[:], 0.0).then_inc(s_id, 1)
                nc.gpsimd.iota(keyno[:], [[1, KEYS]], base=0, channel_multiplier=0,
                               allow_small_or_imprecise_dtypes=True).then_inc(s_id, 1)
                pool.wait_ge(s_c2, 1)
                nc.gpsimd.affine_select(out=ident[:], in_=ident[:], compare_op=ALU.not_equal, fill=1.0, base=0,
                                        pattern=[[-1, P]], channel_multiplier=1).then_inc(s_id, 1)

            @block.scalar
            def _(act):
                act.wait_ge(s_const, 128)
                nc.scalar.activation(gt, gates, ACT.Tanh).then_inc(s_tanh, 1)
                nc.scalar.activation(vw[0][:].rearrange("p k r -> p (k r)"), vraw, ACT.Copy, scale=WS).then_inc(s_tanh, 1)
                for n, (_, rows, cols, dst) in enumerate(SPLIT):
                    act.wait_ge(s_ld[n % NB], 16 * (n // NB + 1))
                    nc.scalar.activation(dst[0], stage[n % NB][0:rows, 0:cols], ACT.Copy, scale=WS).then_inc(s_hi, 1)

                def shift_back(c):
                    act.wait_ge(s_clip, c + 1)
                    if c:
                        act.wait_ge(s_tps, 4 * c)
                    nc.scalar.activation(tern, rounded, ACT.Copy, bias=-ROUND).then_inc(s_tern, 1)
                    for q in range(4):
                        act.wait_ge(s_tps, 4 * c + q + 1)
                        src = bM[q % 2][:].bitcast(F16)[:, 0:512].rearrange("p (k n) -> p k n", k=4)
                        dst = fcw[:, :, (4 * c + q) * P:(4 * c + q + 1) * P] if c < 4 else \
                            prw[:, 4 * q:4 * q + 4, (c - 4) * P:(c - 3) * P]
                        nc.scalar.activation(dst, src, ACT.Copy).then_inc(s_tev, 1)

                for c in range(NTERN):
                    n = NS + c
                    act.wait_ge(s_ld[n % NB], 16 * (n // NB + 1))
                    rows = 4 if c < 4 else 1
                    w = 2048 // rows
                    for q in range(rows):
                        i = 4 * c + q if c < 4 else 12 + c
                        ins = nc.scalar.activation(pt[q % 2][:].rearrange("p h n -> p (h n)") if w == 512 else
                                                   qkt[0][:].rearrange("p h n -> p (h n)"),
                                                   stage[n % NB][:, q * w:(q + 1) * w], ACT.Abs, accum_out=asum[:, i:i + 1])
                        ins.then_inc(s_abs, 1)
                        if q < rows - 1 or c:
                            act.wait_ge(s_abs, min(4 * c, 16) + max(c - 4, 0) + q + 1)
                    if c:
                        shift_back(c - 1)
                shift_back(NTERN - 1)
                for q in range(4):
                    act.wait_ge(s_ups, q + 1)
                    cols = slice(q * 512, (q + 1) * 512)
                    nc.scalar.activation(lru[0:RANK, cols], bM[q % 2][0:RANK, :], ACT.Copy).then_inc(s_uhi, 1)
                    nc.scalar.activation(lru[64:64 + RANK, cols], bM[q % 2][0:RANK, :], ACT.Copy).then_inc(s_uhi, 1)

            @block.vector
            def _(dve):
                vec = nc.vector
                dve.wait_ge(s_id, 6)
                vec.tensor_copy(ident16, ident[:]).then_inc(s_small, 1)
                dve.wait_ge(s_tanh, 2)
                vec.tensor_scalar(gs[:], gt, 1 / WS, None, ALU.mult).then_inc(s_small, 1)
                vec.scalar_tensor_tensor(vw[1][:].rearrange("p k r -> p (k r)"), vraw, WS, vw[0][:].rearrange("p k r -> p (k r)"),
                                         ALU.mult, ALU.subtract).then_inc(s_small, 1)
                for n, (_, rows, cols, dst) in enumerate(SPLIT):
                    dve.wait_ge(s_hi, n + 1)
                    vec.scalar_tensor_tensor(dst[1], stage[n % NB][0:rows, 0:cols], WS, dst[0], ALU.mult, ALU.subtract)\
                        .then_inc(s_lo, 1)
                for c in range(NTERN):
                    rows = 4 if c < 4 else 1
                    w = 2048 // rows
                    i = 4 * c if c < 4 else 12 + c
                    cols = slice(i, i + rows)
                    dve.wait_ge(s_abs, i + rows)
                    vec.tensor_scalar(scale[:, cols], asum[:, cols], 1 / w, 1e-5, ALU.mult, ALU.max).then_inc(s_scale, 1)
                    dve.wait_ge(s_scale, 2 * c + 1)
                    vec.reciprocal(inv[:, cols], scale[:, cols]).then_inc(s_scale, 1)
                    dve.wait_ge(s_scale, 2 * c + 2)
                    if c:
                        dve.wait_ge(s_tern, c)
                    for q in range(rows):
                        ins = vec.tensor_scalar(rounded[:, q * w:(q + 1) * w], stage[(NS + c) % NB][:, q * w:(q + 1) * w],
                                                inv[:, i + q:i + q + 1], ROUND, ALU.mult, ALU.add)
                    ins.then_inc(s_round, 1)
                    dve.wait_ge(s_round, c + 1)
                    vec.tensor_scalar(rounded, rounded, ROUND + 1, ROUND - 1, ALU.min, ALU.max).then_inc(s_clip, 1)
                vec.tensor_copy(fsc[:], scale[:, 0:NM]).then_inc(s_small, 1)
                vec.tensor_tensor(us, u, inv[:, 0:NM].unsqueeze(2).to_broadcast([P, NM, RANK]), ALU.mult).then_inc(s_us, 1)
                dve.wait_ge(s_us, 1)
                vec.tensor_scalar(us, us, gate, None, ALU.mult).then_inc(s_us, 1)
                for j in range(4):
                    if j:
                        dve.wait_ge(s_gps, j)
                    vec.tensor_scalar(diag, ident[:], scale[:, 16 + j:17 + j], None, ALU.mult).then_inc(s_diag, 1)
                for q in range(4):
                    dve.wait_ge(s_uhi, 2 * q + 2)
                    cols = slice(q * 512, (q + 1) * 512)
                    vec.tensor_tensor(lru[32:32 + RANK, cols], bM[q % 2][0:RANK, :], lru[0:RANK, cols], ALU.subtract)\
                        .then_inc(s_ulo, 1)
                dve.wait_ge(s_gps, 4)
                vec.tensor_scalar(gsc[:], bT[0][:], gt[:, 3:4], None, ALU.mult).then_inc(s_g, 1)

            @block.tensor
            def _(pe):
                pe.wait_ge(s_small, 1)
                for c in range(NTERN):
                    pe.wait_ge(s_tern, c + 1)
                    for q in range(4):
                        n = 4 * c + q
                        if n >= 2:
                            pe.wait_ge(s_tev, n - 1)
                        for k in range(4):
                            ins = nc.tensor.transpose(bM[q % 2][:].bitcast(F16)[:, k * P:(k + 1) * P],
                                                      tern[:, (4 * q + k) * P:(4 * q + k + 1) * P], ident16)
                        ins.then_inc(s_tps, 1)
                pe.wait_ge(s_us, 2)
                pe.wait_ge(s_tev, 4 * NTERN)
                for j in range(4):
                    pe.wait_ge(s_diag, j + 1)
                    nc.tensor.matmul(bT[0][:, j * P:(j + 1) * P], ones, diag, start=True, stop=True).then_inc(s_gps, 1)
                for q in range(4):
                    if q >= 2:
                        pe.wait_ge(s_ulo, q - 1)
                    for k in range(4):
                        ins = nc.tensor.transpose(bM[q % 2][0:RANK, k * P:(k + 1) * P], us[:, 4 * q + k, :], ident[:])
                    ins.then_inc(s_ups, 1)

        ld_x, ld_c, ld_s = sem("ld_x"), sem("ld_c"), sem("ld_s")
        cxt_ps, kv_ps, kr_ps, v_ps, kn_ps, krt_ps = (sig("cxt_ps", 1), sig("kv_ps", 1), sig("kr_ps", 1), sig("v_ps", 2),
                                                     sig("kn_ps", NG), sig("krt_ps", 1))
        xt_ps, qc_ps, u_ps, qt_ps = sig("xt_ps", 2 * NT), sig("qc_ps", 2), sig("u_ps", STEPS), sig("qt_ps", STEPS)
        s_ps, pt_ps, o_ps, ao_ps, y_ps = (sig("s_ps", STEPS), sig("pt_ps", STEPS), sig("o_ps", STEPS), sig("ao_ps", 2 * NT),
                                          sig("y_ps", 2 * NT))
        z1_ps, z2_ps, h_ps, m_ps, z_ps = sig("z1_ps", 1), sig("z2_ps", 1), sig("h_ps", NM), sig("m_ps", NM - 1), sig("z_ps", NT)
        cx_hi, kv_hi, kn_hi, kr_hi, v_copy = (sig("cx_hi", 1), sig("kv_hi", 1), sig("kn_hi", NG), sig("kr_hi", 1),
                                              sig("v_copy", 2))
        x_hi, qc_hi, nope, qt_hi = sig("x_hi", 2 * NT), sig("qc_hi", 2), sig("nope", 2 * NT), sig("qt_hi", STEPS)
        e_done, pt_copy, ao_hi, z_hi = sig("e_done", STEPS), sig("pt_copy", STEPS), sig("ao_hi", 2 * NT), sig("z_hi", 1)
        relu_done, sq_done = sig("relu_done", NM), sig("sq_done", NM)
        cx_lo, kv_lo, kn_lo, kr_lo, kr_rope = (sig("cx_lo", 1), sig("kv_lo", 1), sig("kn_lo", NG), sig("kr_lo", 1),
                                               sig("kr_rope", 1))
        x_lo, var_done, xn_done, qc_lo = sig("x_lo", 2 * NT), sig("var_done", 2 * NT), sig("xn_done", 2 * NT), sig("qc_lo", 2)
        rot, qt_lo, masked, top_done, sum_done = (sig("rot", 2 * NT), sig("qt_lo", STEPS), sig("masked", STEPS),
                                                  sig("top_done", STEPS), sig("sum_done", STEPS))
        o_norm, ao_lo, res1 = sig("o_norm", NT), sig("ao_lo", 2 * NT), sig("res1", NT)
        z_copy, z_lo, h_hi, h_lo, y_sc = sig("z_copy", 1), sig("z_lo", 1), sig("h_hi", NM), sig("h_lo", NM), sig("y_sc", NT)
        dv = sig("dv", DVE_LINKS)
        rstd_done, spread, shifted, roped, res2 = (sig("rstd_done", 2 * NT), sig("spread", 1), sig("shifted", STEPS),
                                                   sig("roped", 2 * NT), sig("res2", NT))
        x_out = sig("x_out", 16)

        block = ctx.enter_context(nc.Block())
        S2 = SLOTS + 1
        x_bank = lambda n: n % 2 if n < NT else int(n == 2 * NT - 1)
        Y_SLOT = [10 + 4 * t + (2 if t < NT - 1 else 0) for t in range(NT)]
        y_tiles = lambda s, t: (range(2 * NK) if t == NT - 1 else range(NK) if s == Y_SLOT[t] - 2 else
                                range(NK, NK + 2) if s == Y_SLOT[t] - 1 else range(NK + 2, 2 * NK))
        PIECES_AT = [[0, 1], []] + [[n] for n in range(2, NM)]

        def turns(eng, turn):
            turn(0, None)
            with eng.Fori(0, B - 1) as c:
                turn(c + 1, c)
            turn(None, B - 1)

        bcast = lambda ap, n: ap.unsqueeze(1).to_broadcast([ap.shape[0], n, ap.shape[-1]])

        @block.sync
        def _(sp):
            def load(b):
                sp.dma_start(cx[0:KEYS, :], io["ctx_1024"][b]).then_inc(ld_c, 16)
                sp.dma_start(xin[:], x_v[b]).then_inc(ld_x, 16)
                sp.dma_start(segi[:], io["seg"][b]).then_inc(ld_s, 16)

            def store(b):
                wait(sp, res2, b, NT)
                sp.dma_start(out_v[b], xo[:]).then_inc(x_out.sem, 16)

            load(0)
            with sp.Fori(0, B - 1) as b:
                wait(sp, res1, b, NT)
                load(b + 1)
                store(b)
            store(B - 1)
            sp.wait_ge(x_out.sem, B * 16 + 1)

        @block.gpsimd
        def _(pool):
            prime(pool, [rstd_done, spread, shifted, roped, res2, x_out])
            def turn(b, c):
                def power(n):
                    wait(pool, var_done, b, n + 1)
                    nc.gpsimd.tensor_tensor(rstd[:, n:n + 1], vare[:, n:n + 1], half[:], ALU.pow).then_inc(rstd_done.sem, 1)

                def rotate(n):
                    wait(pool, rot, b, n + 1)
                    if n >= 2:
                        wait(pool, qt_ps, b, 4 * (n // 2) - (2 if n % 2 == 0 else 0))
                    h = slice(8 * (n % 2), 8 * (n % 2) + 8)
                    cs, sn = rm
                    nc.gpsimd.tensor_tensor(qk[:, h, HD:HD + R // 2], cs[:, :, 0, :], sn[:, :, 1, :], ALU.subtract)
                    nc.gpsimd.tensor_tensor(qk[:, h, HD + R // 2:P], sn[:, :, 0, :], cs[:, :, 1, :], ALU.add)\
                        .then_inc(roped.sem, 1)

                if b is not None:
                    for t in range(NT):
                        power(t)
                    wait(pool, kr_lo, b, 1)
                    pool.nop(nofuse=True)
                    for h in range(2):
                        ins = nc.gpsimd.tensor_copy(kc[h][HD:P, 1:H, :], kc[h][HD:P, 0:1, :].to_broadcast([R, H - 1, KEYS]))
                    ins.then_inc(spread.sem, 1)
                    wait(pool, spread, b, 1)
                if c is not None:
                    for t in range(NT):
                        wait(pool, y_sc, c, t + 1)
                        nc.gpsimd.tensor_tensor(xo[:, t, :], xo[:, t, :], xr[:, t, :], ALU.add).then_inc(res2.sem, 1)
                if b is not None:
                    rotate(0)
                    rotate(1)
                    for s in range(S2):
                        if s < STEPS:
                            wait(pool, top_done, b, s + 1)
                            if s >= 3:
                                wait(pool, sum_done, b, s - 2)
                                wait(pool, pt_ps, b, s - 2)
                            nc.gpsimd.tensor_tensor(ex[s % 3][:], sc[s % 2][:],
                                                    smax[:, s % 2, :].unsqueeze(2).to_broadcast([P, HG, KEYS]), ALU.subtract)\
                                .then_inc(shifted.sem, 1)
                        if s % 2 == 1 and s < STEPS - NG:
                            rotate(2 + s // 2)
                        if s - 1 in Y_SLOT:
                            power(NT + Y_SLOT.index(s - 1))

            turns(pool, turn)

        @block.scalar
        def _(act):
            prime(act, [cx_hi, kv_hi, kn_hi, kr_hi, v_copy, x_hi, qc_hi, nope, qt_hi, e_done, pt_copy, ao_hi, z_hi,
                        relu_done, sq_done])
            four = lambda ap: ap.rearrange("p (k n) -> p k n", k=4)
            def turn(b, c):
                def x_high(n):
                    wait(act, xt_ps, b, n + 1)
                    t, u = n % NT, x_bank(n)
                    xt = xta if n < NT else xtb
                    nc.scalar.activation(xt[0][:, :, t * P:(t + 1) * P], four(bT[u][:]), ACT.Copy).then_inc(x_hi.sem, 1)

                def prepare(i):
                    bank = bT[i % 2]
                    if i == 0:
                        wait(act, cxt_ps, b, 1)
                        nc.scalar.activation(cxt[0][:], four(bank[:, 0:NK * KEYS]), ACT.Copy).then_inc(cx_hi.sem, 1)
                    if i == 1:
                        wait(act, kv_ps, b, 1)
                        nc.scalar.activation(kvt[0][:], bank[:, 0:KEYS], ACT.Copy, scale=1 / WS).then_inc(kv_hi.sem, 1)
                    if 2 <= i < 6:
                        x_high(i - 2)
                    if 7 <= i < 9:
                        n = i - 7
                        wait(act, v_ps, b, n + 1)
                        nc.scalar.activation(vc[0:KEYS, n * 512:(n + 1) * 512], bank[0:KEYS, :], ACT.Copy, scale=1 / WS)\
                            .then_inc(v_copy.sem, 1)
                    if 9 <= i < 13:
                        g = i - 9
                        wait(act, kn_ps, b, g + 1)
                        nc.scalar.activation(kc[0][0:HD, g * HG:(g + 1) * HG, :], four(bank[0:HD, 0:HG * KEYS]), ACT.Copy)\
                            .then_inc(kn_hi.sem, 1)
                    if i == 13:
                        wait(act, krt_ps, b, 1)
                        nc.scalar.activation(kc[0][HD:P, 0, :], bank[0:R, 0:KEYS], ACT.Copy).then_inc(kr_hi.sem, 1)
                    if i >= 14:
                        n, rows = i - 14, (P, QR)[i - 14]
                        wait(act, qc_ps, b, n + 1)
                        nc.scalar.activation(qct[0][0:rows, n, :], bank[0:rows, :], ACT.Copy, scale=1 / WS).then_inc(qc_hi.sem, 1)

                def mlp(m):
                    if m == 0:
                        wait(act, z2_ps, c, 1)
                        nc.scalar.activation(lrz[0:RANK, :], bP[0:RANK, :], ACT.Copy)
                        nc.scalar.activation(lrz[32:32 + RANK, :], bP[0:RANK, :], ACT.Copy).then_inc(z_hi.sem, 1)
                        if b is not None:
                            prepare(1)
                    wait(act, h_ps, c, m + 1)
                    if m >= 2:
                        wait(act, h_lo, c, m - 1)
                    nc.scalar.activation(rl[m % 2][:], bM[m % 2][:], ACT.Relu, scale=fsc[:, m:m + 1]).then_inc(relu_done.sem, 1)
                    wait(act, relu_done, c, m + 1)
                    nc.scalar.activation(rl[m % 2][:], rl[m % 2][:], ACT.Square).then_inc(sq_done.sem, 1)

                def nope_copy(n):
                    wait(act, u_ps, b, 2 * n + 1)
                    if n >= 2:
                        wait(act, qt_ps, b, 4 * (n // 2) - (2 if n % 2 == 0 else 0))
                    nc.scalar.activation(qk[:, 8 * (n % 2):8 * (n % 2) + 8, 0:HD], bU[:].rearrange("p (h n) -> p h n", h=8),
                                         ACT.Copy).then_inc(nope.sem, 1)

                def q_high(n):
                    wait(act, qt_ps, b, n + 1)
                    if n >= NG:
                        wait(act, s_ps, b, n - NG + 1)
                    g = n % NG
                    nc.scalar.activation(qkt[0][:, g * HG:(g + 1) * HG, :], four(bT[0][:]), ACT.Copy).then_inc(qt_hi.sem, 1)

                for n in range(NM):
                    if b is not None and n == 0:
                        prepare(0)
                        if c is None:
                            prepare(1)
                    if c is not None:
                        mlp(n)
                    if b is not None and n:
                        for i in PIECES_AT[n]:
                            prepare(i)
                if b is not None:
                    nope_copy(0)
                    nope_copy(1)
                    q_high(0)
                    q_high(1)
                    for s in range(S2):
                        if s % 2 == 0 and s < STEPS - NG:
                            nope_copy(2 + s // 2)
                        if s + 2 < STEPS:
                            q_high(s + 2)
                        if 1 <= s <= STEPS:
                            wait(act, shifted, b, s)
                            e = ex[(s - 1) % 3]
                            nc.scalar.activation(e[:], e[:], ACT.Exp, scale=EXP1).then_inc(e_done.sem, 1)
                        if 2 <= s < STEPS + 2:
                            i = s - 2
                            wait(act, pt_ps, b, i + 1)
                            if i >= 2:
                                wait(act, o_ps, b, i - 1)
                            nc.scalar.activation(pt[i % 2][0:KEYS], four(bP[0:KEYS, :]), ACT.Copy).then_inc(pt_copy.sem, 1)
                        for n in range(2 * NT):
                            if s == 8 + 4 * (n // 2) + n % 2:
                                wait(act, ao_ps, b, n + 1)
                                if n >= 2:
                                    wait(act, y_ps, b, n - 1)
                                nc.scalar.activation(aot[0][:, 4 * (n % 2):4 * (n % 2) + 4, :], four(bT[1][:]), ACT.Copy)\
                                    .then_inc(ao_hi.sem, 1)
                        if s - 4 in Y_SLOT:
                            x_high(NT + Y_SLOT.index(s - 4))

            turns(act, turn)

        @block.tensor
        def _(pe):
            prime(pe, [cxt_ps, kv_ps, kr_ps, v_ps, kn_ps, krt_ps, xt_ps, qc_ps, u_ps, qt_ps, s_ps, pt_ps, o_ps, ao_ps, y_ps,
                       z1_ps, z2_ps, h_ps, m_ps, z_ps])
            mm = nc.tensor.matmul

            def product(out, lhs, rhs, k, n):
                mm(out, lhs(0), rhs(0), start=(k == 0), stop=False)
                mm(out, lhs(0), rhs(1), start=False, stop=False)
                return mm(out, lhs(1), rhs(0), start=False, stop=(k == n - 1))

            def turn(b, c):
                def x_transpose(n):
                    u = x_bank(n)
                    wait(pe, xn_done, b, n + 1)
                    if n == 0:
                        wait(pe, cx_lo, b, 1)
                    elif n == 1:
                        wait(pe, kv_lo, b, 1)
                    elif n < NT:
                        wait(pe, x_lo, b, n - 1)
                    elif u == 1:
                        wait(pe, ao_lo, b, 2 * NT)
                    else:
                        wait(pe, qt_lo, b, STEPS)
                        wait(pe, x_lo, b, n)
                    for k in range(NK):
                        ins = nc.tensor.transpose(bT[u][:, k * P:(k + 1) * P], xn[n % 2][:, k * P:(k + 1) * P], ident[:])
                    ins.then_inc(xt_ps.sem, 1)

                def prepare(i):
                    bank = bT[i % 2]
                    if i == 0:
                        pe.wait_ge(ld_c, b * 16 + 16)
                        if c is not None:
                            wait(pe, x_lo, c, 2 * NT - 1)
                        for k in range(NK):
                            ins = nc.tensor.transpose(bank[:, k * KEYS:(k + 1) * KEYS], cx[0:KEYS, k * P:(k + 1) * P],
                                                      ident[0:KEYS, 0:KEYS])
                        ins.then_inc(cxt_ps.sem, 1)
                    if i == 1:
                        wait(pe, cx_lo, b, 1)
                        wait(pe, x_lo, b, 0)
                        for k in range(NK):
                            ins = product(bank[:, 0:KEYS], lambda h: kvw[h][:, k, :], lambda h: cxt[h][:, k, :], k, NK)
                        ins.then_inc(kv_ps.sem, 1)
                    if 2 <= i < 6:
                        x_transpose(i - 2)
                    if i == 6:
                        wait(pe, x_lo, b, 3)
                        product(bank[0:KEYS, 0:R], lambda h: kvt[h][:], lambda h: krw[h][:], 0, 1).then_inc(kr_ps.sem, 1)
                    if 7 <= i < 9:
                        n = i - 7
                        if n == 0:
                            wait(pe, x_lo, b, 4)
                        else:
                            wait(pe, kr_rope, b, 1)
                        product(bank[0:KEYS, :], lambda h: kvt[h][:], lambda h: vuw[h][:, n * 512:(n + 1) * 512], 0, 1)\
                            .then_inc(v_ps.sem, 1)
                    if 9 <= i < 13:
                        g = i - 9
                        if g < 2:
                            wait(pe, v_copy, b, g + 1)
                        else:
                            wait(pe, kn_lo, b, g - 1)
                        for j in range(HG):
                            col = (g * HG + j) * HD
                            ins = product(bank[0:HD, j * KEYS:(j + 1) * KEYS], lambda h: kuw[h][:, col:col + HD],
                                          lambda h: kvt[h][:], 0, 1)
                        ins.then_inc(kn_ps.sem, 1)
                    if i == 13:
                        wait(pe, kr_rope, b, 1)
                        wait(pe, kn_lo, b, 3)
                        pe.nop(nofuse=True)
                        nc.tensor.transpose(bank[0:R, 0:KEYS], kr[0:KEYS, :], ident[0:KEYS, 0:KEYS]).then_inc(krt_ps.sem, 1)
                    if i >= 14:
                        n, rows = i - 14, (P, QR)[i - 14]
                        if n == 0:
                            wait(pe, kn_lo, b, NG)
                        else:
                            wait(pe, kr_lo, b, 1)
                        for k in range(NK):
                            ins = product(bank[0:rows, :], lambda h: qdw[h][:, k, n * P:n * P + rows],
                                          lambda h: xta[h][:, k, :], k, NK)
                        ins.then_inc(qc_ps.sem, 1)

                def low_rank(m):
                    mm(bM[m % 2][:], lru[0:ZROWS, m * P:(m + 1) * P], lrz[0:ZROWS, :], start=False, stop=True)\
                        .then_inc(h_ps.sem, 1)

                def hidden(m):
                    if m == 0:
                        wait(pe, x_lo, c, 2 * NT)
                        for k in range(NK):
                            ins = product(bU[0:RANK, :], lambda h: vw[h][:, k, :], lambda h: xtb[h][:, k, :], k, NK)
                        ins.then_inc(z1_ps.sem, 1)
                    if m >= 2:
                        wait(pe, relu_done, c, m - 1)
                    for k in range(NK):
                        w = fcw[:, k, m * P:(m + 1) * P]
                        mm(bM[m % 2][:], w, xtb[0][:, k, :], start=(k == 0), stop=False)
                        mm(bM[m % 2][:], w, xtb[1][:, k, :], start=False, stop=False)
                    if m == 0:
                        wait(pe, z_copy, c, 1)
                        pe.nop(nofuse=True)
                        mm(bP[0:RANK, :], fbw[:], zf[:], start=True, stop=True).then_inc(z2_ps.sem, 1)
                    if m == 0:
                        if b is not None:
                            prepare(1)
                        wait(pe, z_lo, c, 1)
                    low_rank(m)

                def output(i):
                    wait(pe, h_lo, c, i + 1)
                    for t in range(NT):
                        mm(acc[t][:], hx[i % 2][0][:, t * P:(t + 1) * P], prw[:, i, :], start=(i == 0), stop=False)
                        ins = mm(acc[t][:], hx[i % 2][1][:, t * P:(t + 1) * P], prw[:, i, :], start=False,
                                 stop=(i == NM - 1))
                        if i == NM - 1:
                            ins.then_inc(z_ps.sem, 1)
                    if i < NM - 1:
                        ins.then_inc(m_ps.sem, 1)

                def project(n):
                    t, r = n // 4, n % 4
                    if n == 0:
                        wait(pe, qc_lo, b, 2)
                        if c is not None:
                            wait(pe, y_sc, c, 1)
                    elif n % 2 == 1:
                        wait(pe, nope, b, n // 2 + 1)
                    else:
                        wait(pe, rot, b, n // 2)
                    product(bU[:], lambda h: qct[h][:, 0, t * P:(t + 1) * P], lambda h: quw[h][:, 0, r, :], 0, 2)
                    tile = qct[0][:, 1, t * P:(t + 1) * P]
                    mm(bU[:], tile, quw[0][:, 1, r, :], start=False, stop=False)
                    mm(bU[:], tile[0:QR, :], quw[1][0:QR, 1, r, :], start=False, stop=True).then_inc(u_ps.sem, 1)

                def q_transpose(n):
                    g = n % 4
                    wait(pe, nope, b, n // 2 + 1)
                    wait(pe, roped, b, n // 2 + 1)
                    if n:
                        wait(pe, qt_lo, b, n)
                    for j in range(HG):
                        ins = nc.tensor.transpose(bT[0][:, j * P:(j + 1) * P], qk[:, g * HG + j, :], ident[:])
                    ins.then_inc(qt_ps.sem, 1)

                for n in range(NM):
                    if b is not None and n == 0:
                        prepare(0)
                        if c is None:
                            prepare(1)
                    if c is not None:
                        hidden(n)
                    if b is not None and n:
                        for i in PIECES_AT[n]:
                            prepare(i)
                    if c is not None and n:
                        output(n - 1)
                if c is not None:
                    output(NM - 1)
                if b is not None:
                    for n in range(4):
                        project(n)
                    q_transpose(0)
                    q_transpose(1)
                    for s in range(S2):
                        if s < STEPS:
                            t, g = s // NG, s % NG
                            if s + 4 < STEPS:
                                project(s + 4)
                            if s == 0:
                                wait(pe, spread, b, 1)
                                if c is not None:
                                    wait(pe, relu_done, c, NM)
                                    wait(pe, y_sc, c, NT)
                            else:
                                wait(pe, masked, b, s)
                            wait(pe, qt_lo, b, s + 1)
                            for j in range(HG):
                                h_ = g * HG + j
                                ins = product(bS[:, j * KEYS:(j + 1) * KEYS], lambda h: qkt[h][:, h_, :], lambda h: kc[h][:, h_, :],
                                              0, 1)
                            ins.then_inc(s_ps.sem, 1)
                        if 2 <= s < STEPS + 2:
                            i = s - 2
                            wait(pe, e_done, b, i + 1)
                            if i:
                                wait(pe, pt_copy, b, i)
                            for j in range(HG):
                                ins = nc.tensor.transpose(bP[0:KEYS, j * P:(j + 1) * P], ex[i % 3][:, j, :], ident[:])
                            ins.then_inc(pt_ps.sem, 1)
                        if s + 2 < STEPS:
                            q_transpose(s + 2)
                        if 3 <= s < STEPS + 3:
                            i = s - 3
                            t, g = i // NG, i % NG
                            wait(pe, pt_copy, b, i + 1)
                            if g == 0:
                                wait(pe, o_norm, b, t)
                                wait(pe, v_copy, b, 2)
                            for j in range(HG):
                                h_ = g * HG + j
                                ins = mm((bO, bY)[h_ // 8][:, (h_ % 8) * HD:(h_ % 8 + 1) * HD], pt[i % 2][0:KEYS, j, :],
                                         vc[0:KEYS, h_ * HD:(h_ + 1) * HD], start=True, stop=True)
                            ins.then_inc(o_ps.sem, 1)
                        for n in range(2 * NT):
                            if s == 8 + 4 * (n // 2) + n % 2:
                                t = n // 2
                                wait(pe, o_norm, b, t + 1)
                                wait(pe, ao_lo, b, n)
                                wait(pe, x_lo, b, NT)
                                for k in range(4):
                                    col = (4 * (n % 2) + k) * P
                                    ins = nc.tensor.transpose(bT[1][:, k * P:(k + 1) * P], ao[:, col:col + P], ident[:])
                                ins.then_inc(ao_ps.sem, 1)
                        for t in range(NT):
                            if Y_SLOT[t] - (2 if t < NT - 1 else 0) <= s <= Y_SLOT[t]:
                                for k in y_tiles(s, t):
                                    if k == 0:
                                        wait(pe, ao_lo, b, 2 * t + 1)
                                        if t:
                                            wait(pe, res1, b, t)
                                    if k == NK:
                                        wait(pe, ao_lo, b, 2 * t + 2)
                                    ins = product(bW[:], lambda h: aot[h][:, k, :], lambda h: ow[h][:, k, :], k, 2 * NK)
                                    if k % NK == NK - 1:
                                        ins.then_inc(y_ps.sem, 1)
                        if s - 3 in Y_SLOT:
                            x_transpose(NT + Y_SLOT.index(s - 3))

            turns(pe, turn)

        @block.vector
        def _(dve):
            vec = nc.vector
            chain = Chain(dv.sem)
            four = lambda ap: ap.rearrange("p (k n) -> p k n", k=4)
            prime(dve, [cx_lo, kv_lo, kn_lo, kr_lo, kr_rope, x_lo, var_done, xn_done, qc_lo, rot, qt_lo, masked, top_done,
                        sum_done, o_norm, ao_lo, res1, z_copy, z_lo, h_hi, h_lo, y_sc, dv])
            def turn(b, c):
                chain.n = 0

                def after(n):
                    wait(dve, dv, b, n)

                def hold(s_, n):
                    wait(dve, s_, b, n)
                    dve.nop(nofuse=True)

                def stats(n, src):
                    i = chain.add(vec.bn_stats(stat[:, n, :], src))
                    hold(dv, i)
                    i = chain.add(vec.bn_aggr(mean[:, n, :], stat[:, n, :]))
                    after(i)
                    vec.tensor_scalar(vare[:, n:n + 1], mean[:, n, 1:2], EPS, None, ALU.add).then_inc(var_done.sem, 1)

                def normalise(n, src):
                    wait(dve, rstd_done, b, n + 1)
                    if n >= 2:
                        wait(dve, xt_ps, b, n - 1)
                    vec.tensor_scalar(xn[n % 2][:], src, mean[:, n, 0:1], rstd[:, n:n + 1], ALU.subtract, ALU.mult)\
                        .then_inc(xn_done.sem, 1)

                def x_low(n):
                    t, u = n % NT, x_bank(n)
                    xt = xta if n < NT else xtb
                    wait(dve, x_hi, b, n + 1)
                    vec.tensor_tensor(xt[1][:, :, t * P:(t + 1) * P], four(bT[u][:]), xt[0][:, :, t * P:(t + 1) * P],
                                      ALU.subtract).then_inc(x_lo.sem, 1)

                def window():
                    dve.wait_ge(ld_s, b * 16 + 16)
                    after(chain.add(vec.tensor_copy(segf[:], segi[:])))
                    for t in range(NT):
                        i = chain.add(vec.tensor_scalar(okay[:, t, :], keyno[:], segf[:, t:t + 1], -float(LOOKBACK),
                                                        ALU.subtract, ALU.is_ge))
                    after(i)
                    for t in range(NT):
                        i = chain.add(vec.scalar_tensor_tensor(pen[:, t, :], keyno[:], segf[:, t:t + 1], okay[:, t, :],
                                                               ALU.is_le, ALU.mult))
                    after(i)
                    return chain.add(vec.tensor_scalar(pen[:], pen[:], -1.0, -LOWEST, ALU.add, ALU.mult))

                def prepare(i):
                    bank = bT[i % 2]
                    if i == 0:
                        wait(dve, cx_hi, b, 1)
                        vec.tensor_tensor(cxt[1][:], four(bank[:, 0:NK * KEYS]), cxt[0][:], ALU.subtract).then_inc(cx_lo.sem, 1)
                    if i == 1:
                        wait(dve, kv_hi, b, 1)
                        vec.scalar_tensor_tensor(kvt[1][:], bank[:, 0:KEYS], 1 / WS, kvt[0][:], ALU.mult, ALU.subtract)\
                            .then_inc(kv_lo.sem, 1)
                    if 2 <= i < 6:
                        x_low(i - 2)
                        if i < 4:
                            normalise(i, xin[:, i, :])
                    if i == 6:
                        wait(dve, kr_ps, b, 1)
                        for q in range(2):
                            n = chain.add(vec.tensor_tensor(krm[0:KEYS, q], bank[0:KEYS, 0:R].rearrange("p (a n) -> p a n", a=2),
                                                            bcast(ktrig[0:KEYS, q, :], 2), ALU.mult))
                        after(n)
                        vec.tensor_tensor(kr[0:KEYS, 0:R // 2], krm[0:KEYS, 0, 0], krm[0:KEYS, 1, 1], ALU.subtract)
                        vec.tensor_tensor(kr[0:KEYS, R // 2:R], krm[0:KEYS, 1, 0], krm[0:KEYS, 0, 1], ALU.add)\
                            .then_inc(kr_rope.sem, 1)
                    if 9 <= i < 13:
                        g = i - 9
                        wait(dve, kn_hi, b, g + 1)
                        hs = slice(g * HG, (g + 1) * HG)
                        vec.tensor_tensor(kc[1][0:HD, hs, :], four(bank[0:HD, 0:HG * KEYS]), kc[0][0:HD, hs, :],
                                          ALU.subtract).then_inc(kn_lo.sem, 1)
                    if i == 13:
                        wait(dve, kr_hi, b, 1)
                        vec.tensor_tensor(kc[1][HD:P, 0, :], bank[0:R, 0:KEYS], kc[0][HD:P, 0, :], ALU.subtract)\
                            .then_inc(kr_lo.sem, 1)
                    if i >= 14:
                        n, rows = i - 14, (P, QR)[i - 14]
                        wait(dve, qc_hi, b, n + 1)
                        low = qct[1][:, 0, :] if n == 0 else qct[0][QR:P, 1, :]
                        vec.scalar_tensor_tensor(low, bank[0:rows, :], 1 / WS, qct[0][0:rows, n, :], ALU.mult,
                                                 ALU.subtract).then_inc(qc_lo.sem, 1)

                def low_rank_side():
                    wait(dve, z1_ps, c, 1)
                    vec.tensor_scalar(zf[:], bU[0:RANK, :], 1 / WS, None, ALU.mult).then_inc(z_copy.sem, 1)
                    wait(dve, z_hi, c, 1)
                    vec.tensor_tensor(lrz[64:64 + RANK, :], bP[0:RANK, :], lrz[0:RANK, :], ALU.subtract).then_inc(z_lo.sem, 1)

                def mlp(m):
                    wait(dve, sq_done, c, m + 1)
                    if m >= 2:
                        wait(dve, m_ps, c, m - 1)
                    vec.tensor_copy(hx[m % 2][0][:], rl[m % 2][:]).then_inc(h_hi.sem, 1)
                    wait(dve, h_hi, c, m + 1)
                    vec.tensor_tensor(hx[m % 2][1][:], rl[m % 2][:], hx[m % 2][0][:], ALU.subtract).then_inc(h_lo.sem, 1)

                def rotate(n):
                    wait(dve, u_ps, b, 2 * n + 2)
                    if n:
                        wait(dve, roped, b, n)
                    for c in range(2):
                        ins = vec.tensor_tensor(rm[c][:].rearrange("p h a n -> p (h a) n"), bU[:].rearrange("p (h n) -> p h n", h=16),
                                                bcast(trig[:, n // 2, c, :], 16), ALU.mult)
                    ins.then_inc(rot.sem, 1)

                def q_low(n):
                    wait(dve, qt_hi, b, n + 1)
                    hs = slice((n % NG) * HG, (n % NG + 1) * HG)
                    vec.tensor_tensor(qkt[1][:, hs, :], four(bT[0][:]), qkt[0][:, hs, :], ALU.subtract).then_inc(qt_lo.sem, 1)

                for n in range(NM):
                    if b is not None and n == 0:
                        prepare(0)
                    if c is not None and n == 0:
                        low_rank_side()
                    if b is not None and n == 0:
                        prepare(1)
                    if c is not None:
                        mlp(n)
                    if b is not None and n < 2:
                        if n == 0:
                            dve.wait_ge(ld_x, b * 16 + 16)
                        for t in (2 * n, 2 * n + 1):
                            stats(t, xin[:, t, :])
                        if n:
                            normalise(0, xin[:, 0, :])
                            normalise(1, xin[:, 1, :])
                    if b is not None and n:
                        for i in PIECES_AT[n]:
                            prepare(i)
                if b is not None:
                    pen_link = window()
                if c is not None:
                    for t in range(NT):
                        wait(dve, z_ps, c, t + 1)
                        if t == 0:
                            dve.wait_ge(x_out.sem, c * 16 + 1)
                        vec.tensor_tensor(xo[:, t, :], acc[t][:], gsc[:], ALU.mult).then_inc(y_sc.sem, 1)
                if b is not None:
                    rotate(0)
                    rotate(1)
                    q_low(0)
                    q_low(1)
                    for s in range(S2):
                        if s % 4 == 3 and 0 <= (s - 7) // 4 < NT:
                            t = (s - 7) // 4
                            wait(dve, sum_done, b, NG * (t + 1))
                            after(chain.add(vec.reciprocal(rinv[:, t, :], rsum[:, t, :])))
                            wait(dve, o_ps, b, NG * (t + 1))
                            if t:
                                wait(dve, ao_ps, b, 2 * t)
                            for n, bank in enumerate((bO, bY)):
                                ins = vec.tensor_tensor(ao[:, n * 512:(n + 1) * 512].rearrange("p (h d) -> p h d", h=8),
                                                        bank[:].rearrange("p (h d) -> p h d", h=8),
                                                        rinv[:, t, 8 * n:8 * n + 8].unsqueeze(2).to_broadcast([P, 8, HD]), ALU.mult)
                            ins.then_inc(o_norm.sem, 1)
                        if s % 2 == 1 and s < STEPS - NG:
                            rotate(2 + s // 2)
                        if s < STEPS:
                            t = s // NG
                            wait(dve, s_ps, b, s + 1)
                            if s >= 2:
                                wait(dve, shifted, b, s - 1)
                            if s == 0:
                                after(pen_link)
                            vec.tensor_tensor(sc[s % 2][:], four(bS[:, 0:HG * KEYS]), bcast(pen[:, t, :], HG), ALU.add)\
                                .then_inc(masked.sem, 1)
                            wait(dve, masked, b, s + 1)
                            vec.tensor_reduce(smax[:, s % 2, :], sc[s % 2][:], AX_X, ALU.max).then_inc(top_done.sem, 1)
                        if s + 2 < STEPS:
                            q_low(s + 2)
                        if 1 <= s <= STEPS:
                            i = s - 1
                            wait(dve, e_done, b, i + 1)
                            vec.tensor_reduce(rsum[:, i // NG, (i % NG) * HG:(i % NG + 1) * HG], ex[i % 3][:], AX_X, ALU.add)\
                                .then_inc(sum_done.sem, 1)
                        for n in range(2 * NT):
                            if s == 8 + 4 * (n // 2) + n % 2:
                                wait(dve, ao_hi, b, n + 1)
                                ks = slice(4 * (n % 2), 4 * (n % 2) + 4)
                                vec.tensor_tensor(aot[1][:, ks, :], four(bT[1][:]), aot[0][:, ks, :], ALU.subtract)\
                                    .then_inc(ao_lo.sem, 1)
                        if s - 1 in Y_SLOT:
                            t = Y_SLOT.index(s - 1)
                            wait(dve, y_ps, b, 2 * t + 2)
                            if t == 0:
                                wait(dve, res2, b, 0)
                            vec.scalar_tensor_tensor(xr[:, t, :], bW[:], gs[:, 1:2], xin[:, t, :], ALU.mult, ALU.add)\
                                .then_inc(res1.sem, 1)
                            wait(dve, res1, b, t + 1)
                            stats(NT + t, xr[:, t, :])
                        if s - 2 in Y_SLOT:
                            t = Y_SLOT.index(s - 2)
                            normalise(NT + t, xr[:, t, :])
                        if s - 4 in Y_SLOT:
                            x_low(NT + Y_SLOT.index(s - 4))
                assert b is None or chain.n == DVE_LINKS, chain.n

            turns(dve, turn)


_INS = ['x', 'ctx_1024', 'g_xattn', 'g_ffn', 'L0_xattn_Wq', 'L0_xattn_bq', 'L0_xattn_Wk', 'L0_xattn_bk',
        'L0_xattn_Wv', 'L0_xattn_bv', 'L0_xattn_Wo', 'L0_xattn_bo', 'w1', 'w2', 'L0_ffn_b1', 'L0_ffn_b2',
        'seg', 'L1_xattn_w_kv_comp', 'L1_xattn_w_q_down', 'quw', 'L1_xattn_w_k_up', 'L1_xattn_w_k_rope',
        'L1_xattn_w_v_up', 'wout', 'L1_ffn_w_fc', 'L1_ffn_w_proj', 'L1_ffn_gate', 'vt', 'u', 'fbt', 'trig', 'ktrig']


def rotary_table(n):
    half = R // 2
    inv = (1.0 / np.power(np.float32(10000.0), np.arange(half, dtype=np.float32) / np.float32(half))).astype(np.float32)
    ang = np.arange(n, dtype=np.float32)[:, None] * inv
    return np.stack([np.cos(ang), np.sin(ang)], axis=1).astype(np.float32)


def kernel(**inputs):
    import concourse.bacc as _bacc
    from concourse.bass_utils import run_bass_kernel_spmd as _run

    a = {k: np.asarray(v) for k, v in inputs.items()}
    for name in ('L0_xattn_Wq', 'L0_xattn_Wk', 'L0_xattn_Wv', 'L0_xattn_Wo'):
        a[name] = a[name].T
    for name in ('L0_xattn_bq', 'L0_xattn_bk'):
        a[name] = a[name].reshape(NG, P).T
    a['L0_ffn_b1'] = a['L0_ffn_b1'].reshape(B, NM, P).transpose(0, 2, 1)
    a['w1'] = a['L0_ffn_w1'].reshape(B, NK, P, NM, P).transpose(0, 3, 2, 1, 4).reshape(B, NM, P, D)
    a['w2'] = a['L0_ffn_w2'].reshape(B, NM, P, D)
    a['seg'] = a['itok_BxS_0_511'].reshape(B, NT, P).transpose(0, 2, 1)
    up, rope = a['L1_xattn_w_q_up'], a['L1_xattn_w_q_rope']
    a['quw'] = np.concatenate([up[:, 0:512], rope[:, 0:512], up[:, 512:1024], rope[:, 512:1024]], axis=1)
    a['quw'] = np.concatenate([a['quw'], a['quw'][P:QC]], axis=0)
    a['wout'] = a['L1_xattn_w_out'].reshape(2 * NK, P, D).transpose(1, 0, 2).reshape(P, 2 * NK * D)
    a['vt'] = a['L1_ffn_v'].T.reshape(NK, P, RANK).transpose(1, 0, 2).reshape(P, NK * RANK)
    a['u'] = a['L1_ffn_u'].reshape(NM, P, RANK).transpose(1, 0, 2)
    a['fbt'] = a['L1_ffn_fast_b'].T
    a['L1_ffn_gate'] = a['L1_ffn_gate'].reshape(1)
    a['trig'] = rotary_table(S).reshape(NT, P, 2, R // 2).transpose(1, 0, 2, 3)
    a['ktrig'] = rotary_table(KEYS)

    nc = _bacc.Bacc("TRN2", target_bir_lowering=False, num_devices=1)
    arrays, io = {}, {}
    for name in _INS:
        arrays[name] = np.ascontiguousarray(a[name])
        io[name] = nc.dram_tensor(name, arrays[name].shape, mybir.dt.from_np(arrays[name].dtype), kind="ExternalInput").ap()
    io["out"] = nc.dram_tensor("out", (B, S, D), F32, kind="ExternalOutput").ap()
    io["mid"] = nc.dram_tensor("mid", (B, S, D), F32, kind="Internal").ap()
    layer0(nc, io)
    layer1(nc, io)
    return _run(nc, [arrays], core_ids=[0]).results[0]["out"]
```
